# Optimizing a Trainium2 kernel written in Bass

```python
import numpy as np
import jax
import jax.numpy as jnp

def _softmax(x, axis=-1):
    return jax.nn.softmax(x, axis=axis)

def _gelu(x):
    return jax.nn.gelu(x, approximate=True)

def _silu(x):
    return jax.nn.silu(x)

def _sigmoid(x):
    return jax.nn.sigmoid(x)

def _layernorm(x, axis=-1, eps=1e-05):
    m = jnp.mean(x, axis=axis, keepdims=True)
    v = jnp.var(x, axis=axis, keepdims=True)
    return (x - m) / jnp.sqrt(v + eps)

def _scatter_add(tgt, idx, src, axis=0):
    return tgt.at[idx].add(src)

def _segment_sum(src, seg, n):
    return jax.ops.segment_sum(src, seg, n)
kernel_name = 'mk_gnn_preln_d2_gnn_r32_5c0287'

def setup_inputs(seed: int=0):
    np.random.seed(seed)
    _w = jnp.asarray

    def _rec_inputs():
        import jax
        import jax.numpy as jnp
        _gk = jax.random.key(seed)
        x = -0.0003713 + 1 * jax.random.normal(jax.random.fold_in(_gk, 1), (3125, 128), jnp.float32)
        _s = jax.random.randint(jax.random.fold_in(_gk, 2), (25000,), 0, 3125, jnp.int32)
        _d = jax.random.randint(jax.random.fold_in(_gk, 3), (25000,), 0, 3125, jnp.int32)
        _loop = jnp.arange(3125, dtype=jnp.int32)
        src = jnp.concatenate([_s, _d, _loop])
        dst = jnp.concatenate([_d, _s, _loop])
        _o = jnp.argsort(dst, stable=True)
        src = src[_o]
        dst = dst[_o]
        edge_attr_128 = -4.21973e-05 + 0.999841 * jax.random.normal(jax.random.fold_in(_gk, 12), (53125, 128), jnp.float32)
        edge_weight = jax.random.uniform(jax.random.fold_in(_gk, 13), (53125,), jnp.float32, 0.0, 1)
        return (x, src, dst, edge_attr_128, edge_weight)
    x, src, dst, edge_attr_128, edge_weight = _rec_inputs()

    def _L0_gnn_setup():
        import jax, jax.numpy as jnp
        import numpy as np
        N_NODES = 3125
        D = 128
        N_EDGES = 50000
        N_LAYERS = 3

        def _spmm(vals, rows, cols, x, n):
            gathered = vals[:, None] * x[cols]
            return jax.ops.segment_sum(gathered, rows, num_segments=n)
        key = jax.random.key(seed)
        k1, k2, k3, k4 = jax.random.split(key, 4)
        emb = jax.random.normal(k1, (N_NODES, D), dtype=jnp.float32)
        vals = jax.random.uniform(k2, (N_EDGES,), dtype=jnp.float32)
        rows = jax.random.randint(k3, (N_EDGES,), 0, N_NODES, dtype=jnp.int64 if jax.config.jax_enable_x64 else jnp.int32)
        cols = jax.random.randint(k4, (N_EDGES,), 0, N_NODES, dtype=jnp.int64 if jax.config.jax_enable_x64 else jnp.int32)
        return {'emb': emb, 'vals': vals, 'rows': rows, 'cols': cols}
    _L0_gnn_all = _L0_gnn_setup()
    _L0_gnn_in = {k: v for k, v in _L0_gnn_all.items() if k in ()}
    del _L0_gnn_all

    def _L1_gnn_setup():
        import jax, jax.numpy as jnp
        import numpy as np
        N_NODES = 50000
        N_EDGES = 18750
        D = 128
        key = jax.random.key(seed)
        k1, k2, k3, k4, k5 = jax.random.split(key, 5)
        node_feats = jax.random.normal(k1, (N_NODES, D), dtype=jnp.float32)
        edge_feats = jax.random.normal(k2, (N_EDGES, D), dtype=jnp.float32)
        mlp_w = jax.random.normal(k3, (D, D), dtype=jnp.float32) * (1.0 / np.sqrt(D))
        mlp_b = jnp.zeros((D,), dtype=jnp.float32)
        scale = jnp.ones((D,), dtype=jnp.float32) * 0.1
        src = jax.random.randint(k4, (N_EDGES,), 0, N_NODES, dtype=jnp.int64)
        dst = jax.random.randint(k5, (N_EDGES,), 0, N_NODES, dtype=jnp.int64)
        return {'node_feats': node_feats, 'edge_feats': edge_feats, 'mlp_w': mlp_w, 'mlp_b': mlp_b, 'scale': scale, 'src': src, 'dst': dst}
    _L1_gnn_all = _L1_gnn_setup()
    _L1_gnn_in = {k: v for k, v in _L1_gnn_all.items() if k in ('mlp_w', 'mlp_b', 'scale')}
    del _L1_gnn_all
    return {'x': x, 'src': src, 'dst': dst, 'edge_attr_128': edge_attr_128, 'edge_weight': edge_weight, 'L1_gnn_mlp_w': _L1_gnn_in['mlp_w'], 'L1_gnn_mlp_b': _L1_gnn_in['mlp_b'], 'L1_gnn_scale': _L1_gnn_in['scale']}

def reference(x, src, dst, edge_attr_128, edge_weight, L1_gnn_mlp_w, L1_gnn_mlp_b, L1_gnn_scale):
    import jax
    import jax.numpy as jnp

    def _L0_gnn_ref(emb, vals, rows, cols):
        import jax, jax.numpy as jnp
        import numpy as np
        N_NODES = 3125
        D = 128
        N_EDGES = 50000
        N_LAYERS = 3

        def _spmm(vals, rows, cols, x, n):
            gathered = vals[:, None] * x[cols]
            return jax.ops.segment_sum(gathered, rows, num_segments=n)
        n = emb.shape[0]
        side = _spmm(vals, rows, cols, emb, n)
        light_out = (emb + N_LAYERS * side) / (N_LAYERS + 1)
        return light_out

    def _L1_gnn_ref(node_feats, edge_feats, mlp_w, mlp_b, scale, src, dst):
        import jax, jax.numpy as jnp
        import numpy as np
        N_NODES = 50000
        N_EDGES = 18750
        D = 128
        n = node_feats.shape[0]
        m = node_feats[src] + edge_feats
        mx = jax.ops.segment_max(m, dst, num_segments=n)
        ex = jnp.exp(m - mx[dst])
        denom = jax.ops.segment_sum(ex, dst, num_segments=n)
        a = ex / denom[dst]
        agg = jax.ops.segment_sum(m * a, dst, num_segments=n)
        h = jax.nn.relu(agg @ mlp_w.T + mlp_b)
        return h * scale + node_feats
    h = jnp.maximum(_layernorm(x, axis=-1), 0.0)
    x = x + _L0_gnn_ref(h, edge_weight, src, dst)
    h = jnp.maximum(_layernorm(x, axis=-1), 0.0)
    x = x + _L1_gnn_ref(h, edge_attr_128, L1_gnn_mlp_w, L1_gnn_mlp_b, L1_gnn_scale, src, dst)
    return x

_drawn_inputs = setup_inputs


def setup_inputs(seed=0):
    import zlib

    import numpy as np

    out = dict(_drawn_inputs(seed))
    spreads = {'L1_gnn_mlp_b': (0.0, 2.0), 'L1_gnn_scale': (0.10000000149011612, 0.6)}
    factors = {'edge_attr_128': 5.235}
    for name, (base, spread) in spreads.items():
        noise = np.random.default_rng([zlib.crc32(name.encode()), seed]).standard_normal(out[name].shape)
        drawn = base * np.exp(spread * noise) if base else spread * noise
        out[name] = jnp.asarray(drawn.astype(out[name].dtype))
    for name, factor in factors.items():
        out[name] = (out[name] * factor).astype(out[name].dtype)
    return out
```

```python
from contextlib import ExitStack

import concourse.bass as bass
from concourse import mybir

F32 = mybir.dt.float32
BF16 = mybir.dt.bfloat16
I32 = mybir.dt.int32
ALU = mybir.AluOpType
ACT = mybir.ActivationFunctionType

P = 128
LANES = 4
GROUP = P * LANES
SLOTS = 8
WINDOW = 64
AHEAD = 4
CHUNK = 4
EPS = 1e-5
BIG = 1.7e38
TINY = 1e-30


def gnn_kernel(nc, x, src, dst, edge_attr, edge_weight, mlp_w, mlp_b, scale, out):
    N, D = x.shape
    E = src.shape[0]
    NBLK = 25
    NP_ = N // NBLK
    assert NP_ * NBLK == N and NP_ <= P and D == P
    G = -(-E // GROUP)
    assert G % SLOTS == 0 and G <= P
    FULL = E // GROUP
    REST = E - FULL * GROUP
    RESTP, RESTJ = REST // LANES, REST % LANES
    assert FULL == G - 1 and REST > 0
    COLS = N + WINDOW
    CHUNKS = [list(range(a, min(a + CHUNK, NBLK))) for a in range(0, NBLK, CHUNK)]
    NCH = len(CHUNKS)

    h_table = nc.dram_tensor("h_table", [N + WINDOW, D], F32, kind="Internal").ap()
    side_tables = [nc.dram_tensor(f"side_table{j}", [N + P, D], F32, kind="Internal").ap()
                   for j in range(LANES)]
    h2_table = nc.dram_tensor("h2_table", [N, D], F32, kind="Internal").ap()

    def blocks(t):
        return t.rearrange("(a p) c -> p a c", p=NP_)

    with ExitStack() as ctx:
        def sb(name, shape, dt=F32):
            return ctx.enter_context(nc.sbuf_tensor(name, shape, dt))

        def psum(name, shape, dt=F32):
            return ctx.enter_context(nc.psum_tensor(name, shape, dt))

        def sem(name):
            return ctx.enter_context(nc.semaphore(name))

        ident = sb("ident", [P, P])
        identb = sb("identb", [P, P], BF16)
        iota_w = sb("iota_w", [P, WINDOW])
        below = sb("below", [P, P])
        spare = sb("spare", [P, 1])
        ones_row = sb("ones_row", [1, P])
        eps_col = sb("eps_col", [P, 1])
        src_g = sb("src_g", [G, GROUP], I32)
        dst_g = sb("dst_g", [G, GROUP], I32)
        prev_g = sb("prev_g", [G, GROUP], I32)
        w_g = sb("w_g", [G, GROUP])
        src_f = sb("src_f", [G, GROUP])
        dst_f = sb("dst_f", [G, GROUP])
        rel_f = sb("rel_f", [G, GROUP])
        same_f = sb("same_f", [G, GROUP])
        cap_g = sb("cap_g", [G, GROUP], BF16)
        lo_i = sb("lo_i", [G, GROUP], I32)
        hi_i = sb("hi_i", [G, GROUP], I32)
        lo_g = sb("lo_g", [G, GROUP], BF16)
        hi_g = sb("hi_g", [G, GROUP], BF16)
        idx_t = sb("idx_t", [P, G + SLOTS, LANES])
        rel_t = sb("rel_t", [P, G, LANES])
        w_t = sb("w_t", [P, G, LANES])
        to_spare = sb("to_spare", [P, G, LANES])
        base_row = sb("base_row", [1, G], I32)
        idx0 = sb("idx0", [P, SLOTS, LANES], I32)
        idx1 = sb("idx1", [P, SLOTS, LANES], I32)
        xs = sb("xs", [NP_, NBLK, D])
        hs = sb("hs", [NP_, NBLK, D])
        rs = sb("rs", [NP_, NBLK, D])
        stats = sb("stats", [NP_, NBLK, 6])
        meanvar = sb("meanvar", [NP_, NBLK, 2])
        std = sb("std", [NP_, NBLK])
        rstd = sb("rstd", [NP_, NBLK])
        shift = sb("shift", [NP_, NBLK])
        acc_t = sb("acc_t", [P, 2, COLS])
        hwin = sb("hwin", [WINDOW, SLOTS, D])
        msg = sb("msg", [P, SLOTS, LANES, D])
        equal = sb("equal", [P, 2, LANES, P])
        earlier = sb("earlier", [P, LANES, P])
        count = sb("count", [P, 2, LANES])
        away = sb("away", [P, 2, LANES])
        oh0 = sb("oh0", [P, 2, LANES, WINDOW])
        ohw = sb("ohw", [P, 2, LANES, WINDOW])
        mix = sb("mix", [WINDOW, 2, LANES, P])
        side_in = sb("side_in", [NP_, 2, LANES, CHUNK, D])
        pair = sb("pair", [NP_, 2, 2, CHUNK, D])
        m = sb("m", [P, SLOTS, LANES, D])
        mt = sb("mt", [P, 2, GROUP])
        mx = sb("mx", [P, 4, GROUP])
        ec = sb("ec", [P, 2, 2, LANES, D])
        oh = sb("oh", [P, 2, LANES, WINDOW])
        drop = sb("drop", [P, 4])
        fac = sb("fac", [P, 4])
        w_sb = sb("w_sb", [D, D])
        w_tr = sb("w_tr", [D, D])
        b_row = sb("b_row", [1, D])
        scale_bc = sb("scale_bc", [P, D])
        tmp = sb("tmp", [NP_, 2, CHUNK, D])

        ps_mt = psum("ps_mt", [P, 2, GROUP])
        ps_cap = psum("ps_cap", [P, 2, GROUP])
        ps_b = psum("ps_b", [P, 2, LANES, D])
        ps_sum = psum("ps_sum", [P, 2, GROUP])

        x_loaded = [sem(f"x_loaded{c}") for c in range(NCH)]
        lists_set = sem("lists_set")
        lists_loaded = sem("lists_loaded")
        w_loaded = sem("w_loaded")
        const_a = sem("const_a")
        const_b = sem("const_b")
        tables_zero = sem("tables_zero")
        stats_done = sem("stats_done")
        aggr_done = sem("aggr_done")
        std_done = sem("std_done")
        rstd_done = sem("rstd_done")
        shift_done = sem("shift_done")
        h_done = sem("h_done")
        xh_done = sem("xh_done")
        h_written = sem("h_written")
        prep_dve = sem("prep_dve")
        prep_pe = sem("prep_pe")
        lists_ready = sem("lists_ready")
        scatter_open = sem("scatter_open")
        gather_open = sem("gather_open")
        zeroed = sem("zeroed")
        tables_cleared = sem("tables_cleared")
        win_loaded = [sem(f"win_loaded{s}") for s in range(SLOTS)]
        src_spread = sem("src_spread")
        equal_done = sem("equal_done")
        oh0_done = sem("oh0_done")
        ohw_done = sem("ohw_done")
        count_done = sem("count_done")
        away_done = sem("away_done")
        idx0_ready = sem("idx0_ready")
        mix_summed = sem("mix_summed")
        mix_done = sem("mix_done")
        msg_summed = sem("msg_summed")
        msg_ready = sem("msg_ready")
        scattered = [sem(f"scattered{j}") for j in range(LANES)]
        side_loaded = [sem(f"side_loaded{c}") for c in range(NCH)]
        pair_done = [sem("pair0_done"), sem("pair1_done")]
        side_done = sem("side_done")
        x1_done = sem("x1_done")
        stats1_done = sem("stats1_done")
        aggr1_done = sem("aggr1_done")
        std1_done = sem("std1_done")
        rstd1_done = sem("rstd1_done")
        shift1_done = sem("shift1_done")
        h2_done = sem("h2_done")
        r_done = sem("r_done")
        h2_written = sem("h2_written")
        idx1_ready = sem("idx1_ready")
        ea_loaded = [sem(f"ea_loaded{s}") for s in range(SLOTS)]
        rest_loaded = sem("rest_loaded")
        m_ready = [sem(f"m_ready{s}") for s in range(SLOTS)]
        mt_done = sem("mt_done")
        evac_done = sem("evac_done")
        scan_done = sem("scan_done")
        rev_done = sem("rev_done")
        drop_done = sem("drop_done")
        fac_done = sem("fac_done")
        b_done = sem("b_done")
        sub_done = sem("sub_done")
        exp_done = sem("exp_done")
        mul_done = sem("mul_done")
        oh_done = sem("oh_done")
        sums_done = sem("sums_done")
        rescaled = sem("rescaled")
        added = sem("added")
        den_done = sem("den_done")
        rec_done = sem("rec_done")
        agg_done = sem("agg_done")
        mlp_done = sem("mlp_done")
        relu_done = sem("relu_done")
        out_done = sem("out_done")
        out_written = sem("out_written")

        block = ctx.enter_context(nc.Block())

        def pipeline(eng, step, lag, peel=1):
            for n in range(SLOTS * peel):
                step(n // SLOTS, n % SLOTS, lambda d, n=n: n - d >= 0)
            with eng.Fori(peel, G // SLOTS) as i:
                for k in range(SLOTS):
                    step(i, k, lambda d: d <= SLOTS * peel)
            for k in range(lag):
                step(G // SLOTS, k, lambda d, k=k: d > k)

        def use(i, k, d=0):
            return i if k >= d else i - 1

        def group(i, k, d=0):
            return i * SLOTS + (k - d)

        @block.sync
        def _(sp):
            for c, ch in enumerate(CHUNKS):
                sp.dma_start(xs[:, ch[0]:ch[-1] + 1, :],
                             blocks(x)[:, ch[0]:ch[-1] + 1, :]).then_inc(x_loaded[c], 16)
            sp.wait_ge(lists_set, 4)
            sp.dma_start(dst_g[0:FULL, :], dst[0:FULL * GROUP].rearrange("(g e) -> g e", e=GROUP)) \
              .then_inc(lists_loaded, 16)
            sp.dma_start(dst_g[FULL:G, 0:REST], dst[FULL * GROUP:E].rearrange("(g e) -> g e", g=1)) \
              .then_inc(lists_loaded, 16)
            sp.dma_start(src_g[0:FULL, :], src[0:FULL * GROUP].rearrange("(g e) -> g e", e=GROUP)) \
              .then_inc(lists_loaded, 16)
            sp.dma_start(src_g[FULL:G, 0:REST], src[FULL * GROUP:E].rearrange("(g e) -> g e", g=1)) \
              .then_inc(lists_loaded, 16)
            sp.dma_start(w_g[0:FULL, :], edge_weight[0:FULL * GROUP].rearrange("(g e) -> g e", e=GROUP)) \
              .then_inc(lists_loaded, 16)
            sp.dma_start(w_g[FULL:G, 0:REST], edge_weight[FULL * GROUP:E].rearrange("(g e) -> g e", g=1)) \
              .then_inc(lists_loaded, 16)
            sp.dma_start(prev_g[0:1, 1:GROUP], dst[0:GROUP - 1].rearrange("(g e) -> g e", g=1)) \
              .then_inc(lists_loaded, 16)
            sp.dma_start(prev_g[1:FULL, :],
                         dst[GROUP - 1:FULL * GROUP - 1].rearrange("(g e) -> g e", e=GROUP)) \
              .then_inc(lists_loaded, 16)
            sp.dma_start(prev_g[FULL:G, 0:REST + 1], dst[FULL * GROUP - 1:E].rearrange("(g e) -> g e", g=1)) \
              .then_inc(lists_loaded, 16)
            sp.dma_start(w_sb[:, :], mlp_w).then_inc(w_loaded, 16)
            sp.dma_start(b_row[:, :], mlp_b.rearrange("(a n) -> a n", a=1)).then_inc(w_loaded, 16)
            sp.dma_start(scale_bc[:, :], scale.rearrange("(a n) -> a n", a=1).to_broadcast([P, D])) \
              .then_inc(w_loaded, 16)
            for c, ch in enumerate(CHUNKS):
                sp.wait_ge(h_done, ch[-1] + 1)
                sp.dma_start(blocks(h_table[0:N, :])[:, ch[0]:ch[-1] + 1, :],
                             hs[:, ch[0]:ch[-1] + 1, :]).then_inc(h_written, 16)

            sp.wait_ge(zeroed, 1)
            sp.dma_start(h_table[N:N + WINDOW, :], rs[0:WINDOW, 0, :]).then_inc(tables_cleared, 16)
            for t in side_tables:
                sp.dma_start(blocks(t[0:N, :]), rs[:, :, :]).then_inc(tables_cleared, 16)
                sp.dma_start(t[N:N + P, :].rearrange("(p a) c -> p a c", a=2), rs[0:P // 2, 0:2, :]) \
                  .then_inc(tables_cleared, 16)

            def load_group(slot, rows):
                sp.dma_start(m[:, slot, :, :], rows.rearrange("(p j) c -> p j c", j=LANES)) \
                  .then_inc(ea_loaded[slot], 16)

            for s in range(SLOTS):
                load_group(s, edge_attr[s * GROUP:(s + 1) * GROUP, :])

            sp.wait_ge(h_written, 16 * NCH)
            sp.wait_ge(tables_cleared, 16 * (1 + 2 * LANES))
            sp.wait_ge(lists_ready, 2)

            def load_window(i, k, live):
                g = group(i, k)
                if live(SLOTS):
                    sp.wait_ge(msg_summed, g - SLOTS + 1)
                start = sp.value_load(base_row[0:1, bass.ds(g, 1)], min_val=0, max_val=N - 1)
                sp.dma_start(hwin[:, k, :], h_table[bass.ds(start, WINDOW), :]).then_inc(win_loaded[k], 16)

            pipeline(sp, load_window, 0)

            for j in range(LANES):
                sp.wait_ge(scattered[j], 16 * G)
            for c, ch in enumerate(CHUNKS):
                if c >= 2:
                    sp.wait_ge(side_done, c - 1)
                for j, t in enumerate(side_tables):
                    sp.dma_start(side_in[:, c % 2, j, 0:len(ch), :],
                                 blocks(t[0:N, :])[:, ch[0]:ch[-1] + 1, :]).then_inc(side_loaded[c], 16)
            for c, ch in enumerate(CHUNKS):
                sp.wait_ge(h2_done, ch[-1] + 1)
                sp.dma_start(blocks(h2_table)[:, ch[0]:ch[-1] + 1, :],
                             hs[:, ch[0]:ch[-1] + 1, :]).then_inc(h2_written, 16)
            with sp.Fori(1, G // SLOTS - 1) as i:
                for k in range(SLOTS):
                    sp.wait_ge(mul_done, (i - 1) * SLOTS + k + 1)
                    load_group(k, edge_attr[bass.ds((i * SLOTS + k) * GROUP, GROUP), :])
            for k in range(SLOTS):
                g = G - SLOTS + k
                sp.wait_ge(mul_done, g - SLOTS + 1)
                if g < FULL:
                    load_group(k, edge_attr[g * GROUP:(g + 1) * GROUP, :])
                else:
                    rows = edge_attr[g * GROUP:g * GROUP + RESTP * LANES, :]
                    sp.dma_start(m[0:RESTP, k, :, :], rows.rearrange("(p j) c -> p j c", j=LANES)) \
                      .then_inc(ea_loaded[k], 16)
                    sp.dma_start(m[RESTP:RESTP + 1, k, 0:RESTJ, :],
                                 edge_attr[E - RESTJ:E, :].rearrange("(p j) c -> p j c", j=RESTJ)) \
                      .then_inc(rest_loaded, 16)
            for c, ch in enumerate(CHUNKS):
                sp.wait_ge(out_done, c + 1)
                sp.dma_start(blocks(out)[:, ch[0]:ch[-1] + 1, :],
                             rs[:, ch[0]:ch[-1] + 1, :]).then_inc(out_written, 16)
            sp.wait_ge(out_written, 16 * NCH)

        @block.gpsimd
        def _(pool):
            nc.gpsimd.memset(dst_g[:, :], -1).then_inc(lists_set, 1)
            nc.gpsimd.memset(prev_g[:, :], -1).then_inc(lists_set, 1)
            nc.gpsimd.memset(src_g[:, :], 0).then_inc(lists_set, 1)
            nc.gpsimd.memset(w_g[:, :], 0.0).then_inc(lists_set, 1)
            nc.gpsimd.memset(ident[:, :], 0.0).then_inc(const_a, 1)
            nc.gpsimd.memset(identb[:, :], 0.0).then_inc(const_a, 1)
            nc.gpsimd.iota(iota_w[:, :], pattern=[[1, WINDOW]], base=0, channel_multiplier=0,
                           allow_small_or_imprecise_dtypes=True).then_inc(const_b, 1)
            pool.wait_ge(const_a, 2)
            for t in (ident, identb):
                nc.gpsimd.affine_select(out=t[:, :], in_=t[:, :], compare_op=ALU.not_equal, fill=1.0, base=0,
                                        pattern=[[-1, P]], channel_multiplier=1).then_inc(const_b, 1)
            nc.gpsimd.memset(ones_row[:, :], 1.0).then_inc(const_b, 1)
            nc.gpsimd.memset(rs[:, :, :], 0.0).then_inc(zeroed, 1)
            nc.gpsimd.memset(below[:, :], 1.0).then_inc(const_a, 1)
            nc.gpsimd.iota(spare[:, :], pattern=[[1, 1]], base=N, channel_multiplier=1,
                           allow_small_or_imprecise_dtypes=True).then_inc(const_a, 1)
            pool.wait_ge(const_a, 4)
            nc.gpsimd.affine_select(out=below[:, :], in_=below[:, :], compare_op=ALU.is_gt, fill=0.0, base=0,
                                    pattern=[[-1, P]], channel_multiplier=1).then_inc(const_a, 1)
            nc.gpsimd.memset(acc_t[:, :, :], 0.0).then_inc(tables_zero, 1)
            nc.gpsimd.memset(idx_t[:, G:G + SLOTS, :], 0.0).then_inc(tables_zero, 1)


            def scatter0(i, k, live):
                pool.wait_ge(msg_ready, group(i, k) + 1)
                pool.wait_ge(idx0_ready, group(i, k) + 1)
                for j in range(LANES):
                    if live(1):
                        pool.wait_ge(scattered[j], group(i, k) * 16)
                    pool.sem_inc(scatter_open, 1)
                    nc.gpsimd.indirect_dma_start(
                        side_tables[j][:, :], bass.IndirectOffsetOnAxis(ap=idx0[:, k, j:j + 1], axis=0),
                        msg[:, k, j, :], None, compute_op=ALU.add).then_inc(scattered[j], 16)

            pool.wait_ge(tables_cleared, 16 * (1 + 2 * LANES))
            pipeline(pool, scatter0, 0)

            for c, ch in enumerate(CHUNKS):
                a1 = len(ch)
                pool.wait_ge(side_loaded[c], 16 * LANES)
                if c >= 2:
                    pool.wait_ge(side_done, c - 1)
                nc.gpsimd.tensor_tensor(pair[:, c % 2, 1, 0:a1, :], side_in[:, c % 2, 2, 0:a1, :],
                                        side_in[:, c % 2, 3, 0:a1, :], ALU.add).then_inc(pair_done[1], 1)
            pool.wait_ge(h2_written, 16 * NCH)

            def gather1(i, k, live):
                pool.wait_ge(idx1_ready, group(i, k) + 1)
                pool.wait_ge(ea_loaded[k], (i + 1) * 16)
                pool.sem_inc(gather_open, 1)
                for j in range(LANES):
                    nc.gpsimd.indirect_dma_start(
                        m[:, k, j, :], None, h2_table[:, :],
                        bass.IndirectOffsetOnAxis(ap=idx1[:, k, j:j + 1], axis=0),
                        compute_op=ALU.add).then_inc(m_ready[k], 16)

            pipeline_last = G // SLOTS - 1
            for k in range(SLOTS):
                gather1(0, k, None)
            with pool.Fori(1, pipeline_last) as i:
                for k in range(SLOTS):
                    gather1(i, k, None)
            for k in range(SLOTS):
                if k == SLOTS - 1:
                    pool.wait_ge(rest_loaded, 16)
                gather1(pipeline_last, k, None)

        @block.scalar
        def _(act):
            def normalize(stat_sem, std_sem, shift_sem, done):
                for c, ch in enumerate(CHUNKS):
                    a0, a1 = ch[0], ch[-1] + 1
                    act.wait_ge(stat_sem, a1)
                    nc.scalar.activation(std[:, a0:a1], meanvar[:, a0:a1, 1], ACT.Sqrt,
                                         bias=eps_col[0:NP_, 0:1]).then_inc(std_sem, 1)
                    act.wait_ge(shift_sem, c + 1)
                    for a in ch:
                        nc.scalar.activation(hs[:, a, :], xs[:, a, :], ACT.Relu, bias=shift[:, a:a + 1],
                                             scale=rstd[:, a:a + 1]).then_inc(done, 1)

            act.wait_ge(const_b, 5)
            normalize(aggr_done, std_done, shift_done, h_done)

            def mix_and_messages(i, k, live):
                if live(1):
                    g, b = group(i, k, 1), (k - 1) % 2
                    pe_done = mix_summed
                    act.wait_ge(pe_done, g + 1)
                    if live(3):
                        act.wait_ge(msg_summed, g - 1)
                    nc.scalar.copy(mix[:, b, :, :], ps_mt[0:WINDOW, b, :].rearrange("d (j e) -> d j e", j=LANES)) \
                      .then_inc(mix_done, 1)
                if live(2):
                    g, b = group(i, k, 2), k % 2
                    act.wait_ge(msg_summed, g + 1)
                    if live(2 + SLOTS):
                        for j in range(LANES):
                            act.wait_ge(scattered[j], (g - SLOTS + 1) * 16)
                    nc.scalar.copy(msg[:, (k - 2) % SLOTS, :, :], ps_b[:, b, :, :]).then_inc(msg_ready, 1)

            pipeline(act, mix_and_messages, 2, peel=2)

            act.wait_ge(lists_ready, 2)
            for s in range(AHEAD):
                nc.scalar.copy(idx1[:, s, :], idx_t[:, s, :]).then_inc(idx1_ready, 1)
            act.wait_ge(h_written, 16 * NCH)
            normalize(aggr1_done, std1_done, shift1_done, h2_done)

            def stage(i, k, live):
                s = (k + AHEAD) % SLOTS
                if live(SLOTS - AHEAD):
                    act.wait_ge(m_ready[s], (use(i, k, SLOTS - AHEAD) + 1) * 16 * LANES)
                nc.scalar.copy(idx1[:, s, :], idx_t[:, bass.ds(group(i, k) + AHEAD, 1), :]
                               .rearrange("p a j -> p (a j)")).then_inc(idx1_ready, 1)

            def step(i, k, live):
                if live(2):
                    g = group(i, k, 2)
                    act.wait_ge(sub_done, g + 1)
                    e = ec[:, k % 2, 0, :, :]
                    nc.scalar.activation(e, e, ACT.Exp).then_inc(exp_done, 1)
                if live(0):
                    g = group(i, k)
                    act.wait_ge(mt_done, g + 1)
                    if live(2):
                        act.wait_ge(scan_done, g - 1)
                    nc.scalar.copy(mt[:, k % 2, :], ps_mt[:, k % 2, :]).then_inc(evac_done, 1)
                    stage(i, k, live)
                if live(1):
                    g, c = group(i, k, 1), (k - 1) % 4
                    act.wait_ge(drop_done, g + 1)
                    if live(5):
                        act.wait_ge(added, g - 3)
                    nc.scalar.activation(fac[:, c:c + 1], drop[:, c:c + 1], ACT.Exp).then_inc(fac_done, 1)

            pipeline(act, step, 2)

        @block.tensor
        def _(pe):
            pe.wait_ge(const_b, 4)
            for n, (t, ready) in enumerate(((src_f, 1), (rel_f, 5), (w_g, 0))):
                if ready:
                    pe.wait_ge(prep_dve, ready)
                else:
                    pe.wait_ge(lists_loaded, 16 * 9)
                bank = ps_mt[:, n, :] if n < 2 else ps_cap[:, 0, :]
                for j in range(LANES):
                    pe.transpose(bank[:, j * G:(j + 1) * G], t[:, j::LANES], ident[0:G, 0:G]) \
                      .then_inc(prep_pe, 1)
            pe.transpose(ps_cap[0:1, 1, 0:G], dst_f[:, 0:1], ident[0:G, 0:G]).then_inc(prep_pe, 1)
            pe.wait_ge(w_loaded, 16 * 3)
            pe.transpose(ps_b[:, 0, 0, :], w_sb[:, :], ident[:, :]).then_inc(prep_pe, 1)

            pe.wait_ge(prep_dve, 13)

            def messages(i, k, live):
                if live(0):
                    g, b = group(i, k), k % 2
                    if live(2):
                        pe.wait_ge(equal_done, g - 1)
                    pick = identb[0:G, bass.ds(g, 1)].to_broadcast([G, P])
                    pe.matmul(ps_cap[:, b, :], pick, hi_g[:, :], start=True, stop=False)
                    pe.matmul(ps_cap[:, b, :], pick, lo_g[:, :], start=False, stop=True) \
                      .then_inc(src_spread, 1)
                if live(1):
                    g, b = group(i, k, 1), (k - 1) % 2
                    pe.wait_ge(equal_done, g + 1)
                    pe.wait_ge(ohw_done, g + 1)
                    if live(3):
                        pe.wait_ge(mix_done, g - 1)
                    for j in range(LANES):
                        mm = pe.matmul(ps_mt[0:WINDOW, b, j * P:(j + 1) * P], ohw[:, b, j, :],
                                       equal[:, b, j, :], start=True, stop=True)
                    mm.then_inc(mix_summed, 1)
                if live(2):
                    g, b = group(i, k, 2), k % 2
                    pe.wait_ge(mix_done, g + 1)
                    pe.wait_ge(win_loaded[(k - 2) % SLOTS], (use(i, k, 2) + 1) * 16)
                    if live(4):
                        pe.wait_ge(msg_ready, g - 1)
                    for j in range(LANES):
                        mm = pe.matmul(ps_b[:, b, j, :], mix[:, b, j, :], hwin[:, (k - 2) % SLOTS, :],
                                       start=True, stop=True)
                    mm.then_inc(msg_summed, 1)

            pipeline(pe, messages, 2)
            pe.wait_ge(msg_ready, G)

            def step(i, k, live):
                if live(0):
                    g, b = group(i, k), k % 2
                    pe.wait_ge(m_ready[k], (i + 1) * 16 * LANES)
                    if live(2):
                        pe.wait_ge(evac_done, g - 1)
                    if live(2):
                        pe.wait_ge(rev_done, g - 1)
                    for j in range(LANES):
                        pe.transpose(ps_mt[:, b, j::LANES], m[:, k, j, :], ident[:, :])
                    pick = identb[0:G, bass.ds(g, 1)].to_broadcast([G, P])
                    pe.matmul(ps_cap[:, b, :], pick, cap_g[:, :], start=True, stop=True) \
                      .then_inc(mt_done, 1)
                if live(1):
                    g, b = group(i, k, 1), (k - 1) % 2
                    pe.wait_ge(rev_done, g + 1)
                    if live(3):
                        pe.wait_ge(sub_done, g - 1)
                    for j in range(LANES):
                        mm = pe.transpose(ps_b[:, b, j, :], mx[:, (k - 1) % 4, j::LANES], ident[:, :])
                    mm.then_inc(b_done, 1)
                if live(2):
                    g, b = group(i, k, 2), k % 2
                    pe.wait_ge(mul_done, g + 1)
                    pe.wait_ge(oh_done, g + 1)
                    if live(4):
                        pe.wait_ge(added, g - 1)
                    for q in range(2):
                        for j in range(LANES):
                            mm = pe.matmul(ps_sum[:, b, q * WINDOW:(q + 1) * WINDOW], ec[:, b, q, j, :],
                                           oh[:, b, j, :], start=(j == 0), stop=(j == LANES - 1))
                    mm.then_inc(sums_done, 1)

            pipeline(pe, step, 2)

            for c, ch in enumerate(CHUNKS):
                pe.wait_ge(agg_done, c + 1)
                if c >= 2:
                    pe.wait_ge(relu_done, c - 1)
                for q, a in enumerate(ch):
                    o = ps_mt[0:NP_, c % 2, q * D:(q + 1) * D]
                    pe.matmul(o, acc_t[:, 1, a * NP_:(a + 1) * NP_], w_tr[:, :], start=True, stop=False)
                    mm = pe.matmul(o, ones_row[:, 0:NP_], b_row[:, :], start=False, stop=True)
                mm.then_inc(mlp_done, 1)

        @block.vector
        def _(dve):
            nc.vector.memset(eps_col[:, :], EPS).then_inc(const_b, 1)

            def norm_stats(c, ch, stats_sem, aggr_sem, std_sem, rstd_sem, shift_sem):
                a0, a1 = ch[0], ch[-1] + 1
                for a in ch:
                    nc.vector.bn_stats(stats[:, a, :], xs[:, a, :]).then_inc(stats_sem, 1)
                dve.wait_ge(stats_sem, a1)
                for a in ch:
                    nc.vector.bn_aggr(meanvar[:, a, :], stats[:, a, :]).then_inc(aggr_sem, 1)
                dve.wait_ge(std_sem, c + 1)
                nc.vector.reciprocal(rstd[:, a0:a1], std[:, a0:a1]).then_inc(rstd_sem, 1)
                dve.wait_ge(rstd_sem, c + 1)
                nc.vector.scalar_tensor_tensor(out=shift[:, a0:a1], in0=meanvar[:, a0:a1, 0], scalar=-1.0,
                                               in1=rstd[:, a0:a1], op0=ALU.mult, op1=ALU.mult) \
                  .then_inc(shift_sem, 1)

            for c, ch in enumerate(CHUNKS):
                dve.wait_ge(x_loaded[c], 16)
                norm_stats(c, ch, stats_done, aggr_done, std_done, rstd_done, shift_done)

            dve.wait_ge(lists_loaded, 16 * 9)
            nc.vector.tensor_copy(src_f[:, :], src_g[:, :]).then_inc(prep_dve, 1)
            nc.vector.tensor_copy(dst_f[:, :], dst_g[:, :]).then_inc(prep_dve, 1)
            nc.vector.tensor_tensor(same_f[:, :], dst_g[:, :], prev_g[:, :], ALU.is_equal).then_inc(prep_dve, 1)
            dve.wait_ge(prep_dve, 3)
            nc.vector.tensor_scalar(cap_g[:, :], same_f[:, :], 2 * BIG, -BIG, ALU.mult, ALU.add) \
              .then_inc(prep_dve, 1)
            nc.vector.tensor_scalar(rel_f[:, :], dst_f[:, :], dst_f[:, 0:1], None, ALU.subtract) \
              .then_inc(prep_dve, 1)

            nc.vector.tensor_scalar(lo_i[:, :], src_g[:, :], WINDOW - 1, None, ALU.bitwise_and) \
              .then_inc(prep_dve, 1)
            nc.vector.tensor_scalar(hi_i[:, :], src_g[:, :], -WINDOW, None, ALU.bitwise_and) \
              .then_inc(prep_dve, 1)
            dve.wait_ge(prep_dve, 7)
            nc.vector.tensor_copy(lo_g[:, :], lo_i[:, :]).then_inc(prep_dve, 1)
            nc.vector.tensor_copy(hi_g[:, :], hi_i[:, :]).then_inc(prep_dve, 1)

            def turned(bank):
                return bank[:, 0:LANES * G].rearrange("p (j g) -> p g j", j=LANES)

            dve.wait_ge(prep_pe, 4)
            nc.vector.tensor_copy(idx_t[:, 0:G, :], turned(ps_mt[:, 0, :])).then_inc(lists_ready, 1)
            dve.wait_ge(tables_zero, 2)
            dve.wait_ge(prep_pe, 8)
            nc.vector.tensor_copy(rel_t[:, :, :], turned(ps_mt[:, 1, :])).then_inc(prep_dve, 1)
            dve.wait_ge(prep_pe, 12)
            nc.vector.tensor_copy(w_t[:, :, :], turned(ps_cap[:, 0, :])).then_inc(prep_dve, 1)
            dve.wait_ge(prep_pe, 13)
            nc.vector.tensor_copy(base_row[:, :], ps_cap[0:1, 1, 0:G]).then_inc(lists_ready, 1)
            dve.wait_ge(prep_pe, 14)
            nc.vector.tensor_copy(w_tr[:, :], ps_b[:, 0, 0, :]).then_inc(prep_dve, 1)
            dve.wait_ge(lists_ready, 2)
            dve.wait_ge(h_done, NBLK)
            dve.wait_ge(const_a, 5)
            nc.vector.scalar_tensor_tensor(out=xs[:, :, :], in0=hs[:, :, :], scalar=0.25, in1=xs[:, :, :],
                                           op0=ALU.mult, op1=ALU.add).then_inc(prep_dve, 1)
            nc.vector.tensor_scalar(to_spare[:, :, :], idx_t[:, 0:G, :], -1.0, spare[:, 0:1], ALU.mult, ALU.add) \
              .then_inc(prep_dve, 1)
            dve.wait_ge(prep_dve, 14)

            lanes = [P, LANES, WINDOW]

            def window_match(o, i, k, d, done):
                nc.vector.tensor_tensor(o, iota_w[:, :].rearrange("p (a w) -> p a w", a=1).to_broadcast(lanes),
                                        rel_t[:, bass.ds(group(i, k, d), 1), :]
                                        .rearrange("p a j -> p j a").to_broadcast(lanes),
                                        ALU.is_equal).then_inc(done, 1)

            def window_start(i, k, d):
                return dve.value_load(base_row[0:1, bass.ds(group(i, k, d), 1)], min_val=0, max_val=N - 1)

            def step0(i, k, live):
                g, b = group(i, k), k % 2
                dve.wait_ge(src_spread, g + 1)
                if live(2):
                    dve.wait_ge(mix_summed, g - 1)
                nc.vector.tensor_tensor(equal[:, b, :, :],
                                        ps_cap[:, b, :].rearrange("p (e j) -> p j e", j=LANES),
                                        idx_t[:, bass.ds(g, 1), :].rearrange("p a j -> p j a")
                                        .to_broadcast([P, LANES, P]), ALU.is_equal).then_inc(equal_done, 1)
                window_match(oh0[:, b, :, :], i, k, 0, oh0_done)
                dve.wait_ge(equal_done, g + 1)
                for j in range(LANES):
                    nc.vector.tensor_tensor_reduce(earlier[:, j, :], equal[:, b, j, :], below[:, :], 1.0, 0.0,
                                                   ALU.mult, ALU.add, count[:, b, j:j + 1]) \
                      .then_inc(count_done, 1)
                dve.wait_ge(oh0_done, g + 1)
                nc.vector.tensor_tensor(ohw[:, b, :, :], oh0[:, b, :, :],
                                        w_t[:, bass.ds(g, 1), :].rearrange("p a j -> p j a")
                                        .to_broadcast(lanes), ALU.mult).then_inc(ohw_done, 1)
                dve.wait_ge(count_done, (g + 1) * LANES)
                nc.vector.scalar_tensor_tensor(out=away[:, b, :], in0=count[:, b, :], scalar=1.0,
                                               in1=to_spare[:, bass.ds(g, 1), :].rearrange("p a j -> p (a j)"),
                                               op0=ALU.min, op1=ALU.mult).then_inc(away_done, 1)
                if live(SLOTS):
                    for j in range(LANES):
                        dve.wait_ge(scattered[j], (g - SLOTS + 1) * 16)
                dve.wait_ge(away_done, g + 1)
                nc.vector.tensor_tensor(idx0[:, k, :], away[:, b, :],
                                        idx_t[:, bass.ds(g, 1), :].rearrange("p a j -> p (a j)"),
                                        ALU.add).then_inc(idx0_ready, 1)

            pipeline(dve, step0, 0)

            for c, ch in enumerate(CHUNKS):
                a0, a1 = ch[0], ch[-1] + 1
                n = a1 - a0
                dve.wait_ge(side_loaded[c], 16 * LANES)
                both = [pair[:, c % 2, q, 0:n, :] for q in range(2)]
                nc.vector.tensor_tensor(both[0], side_in[:, c % 2, 0, 0:n, :], side_in[:, c % 2, 1, 0:n, :],
                                        ALU.add).then_inc(pair_done[0], 1)
                dve.wait_ge(pair_done[0], c + 1)
                dve.wait_ge(pair_done[1], c + 1)
                nc.vector.tensor_tensor(both[0], both[0], both[1], ALU.add).then_inc(side_done, 1)
                dve.wait_ge(side_done, c + 1)
                nc.vector.scalar_tensor_tensor(out=xs[:, a0:a1, :], in0=both[0], scalar=0.75,
                                               in1=xs[:, a0:a1, :], op0=ALU.mult, op1=ALU.add) \
                  .then_inc(x1_done, 1)
                dve.wait_ge(x1_done, c + 1)
                norm_stats(c, ch, stats1_done, aggr1_done, std1_done, rstd1_done, shift1_done)
            dve.wait_ge(h2_done, NBLK)
            nc.vector.tensor_tensor(rs[:, :, :], xs[:, :, :], hs[:, :, :], ALU.add).then_inc(r_done, 1)

            def step(i, k, live):
                if live(2):
                    g, b = group(i, k, 2), k % 2
                    dve.wait_ge(b_done, g + 1)
                    if live(4):
                        dve.wait_ge(sums_done, g - 1)
                    nc.vector.tensor_tensor(ec[:, b, 0, :, :], m[:, (k - 2) % SLOTS, :, :], ps_b[:, b, :, :],
                                            ALU.subtract).then_inc(sub_done, 1)
                if live(1):
                    g, b = group(i, k, 1), (k - 1) % 2
                    now = mx[:, (k - 1) % 4, :]
                    dve.wait_ge(evac_done, g + 1)
                    if live(5):
                        dve.wait_ge(b_done, g - 3)
                    before = mx[:, (k - 2) % 4, GROUP - 1:GROUP] if live(2) else -BIG
                    nc.vector.tensor_tensor_scan(now, ps_cap[:, b, :], mt[:, b, :], before,
                                                 ALU.min, ALU.max).then_inc(scan_done, 1)
                if live(2):
                    window_match(oh[:, k % 2, :, :], i, k, 2, oh_done)
                if live(1):
                    dve.wait_ge(scan_done, g + 1)
                    back = mx[:, (k - 1) % 4, GROUP - 2::-1]
                    nc.vector.tensor_tensor_scan(back, ps_cap[:, b, GROUP - 1:0:-1], back,
                                                 mx[:, (k - 1) % 4, GROUP - 1:GROUP], ALU.min, ALU.max) \
                      .then_inc(rev_done, 1)
                if live(2):
                    b2 = k % 2
                    dve.wait_ge(exp_done, group(i, k, 2) + 1)
                    nc.vector.tensor_tensor(ec[:, b2, 1, :, :], m[:, (k - 2) % SLOTS, :, :],
                                            ec[:, b2, 0, :, :], ALU.mult).then_inc(mul_done, 1)
                if live(1):
                    c = (k - 1) % 4
                    dve.wait_ge(rev_done, g + 1)
                    if live(5):
                        dve.wait_ge(fac_done, g - 3)
                    first = mx[:, c, 0:1]
                    nc.vector.scalar_tensor_tensor(out=drop[:, c:c + 1], in0=first,
                                                   scalar=(mx[:, (k - 2) % 4, GROUP - 1:GROUP] if live(2)
                                                           else 0.0),
                                                   in1=first, op0=ALU.min, op1=ALU.subtract) \
                      .then_inc(drop_done, 1)
                if live(3):
                    g, b, c = group(i, k, 3), (k - 3) % 2, (k - 3) % 4
                    start = window_start(i, k, 3)
                    dve.wait_ge(fac_done, g + 1)
                    if live(4):
                        dve.wait_ge(added, g)
                    head = acc_t[:, :, bass.ds(start, 1)]
                    nc.vector.tensor_scalar(head, head, fac[:, c:c + 1], None, ALU.mult).then_inc(rescaled, 1)
                    dve.wait_ge(rescaled, g + 1)
                    dve.wait_ge(sums_done, g + 1)
                    cols = acc_t[:, :, bass.ds(start, WINDOW)]
                    nc.vector.tensor_tensor(cols, cols, ps_sum[:, b, 0:2 * WINDOW]
                                            .rearrange("p (q w) -> p q w", q=2), ALU.add).then_inc(added, 1)

            pipeline(dve, step, 3)

            dve.wait_ge(added, G)
            dve.wait_ge(r_done, 1)
            for c, ch in enumerate(CHUNKS):
                n0, n1 = ch[0] * NP_, (ch[-1] + 1) * NP_
                nc.vector.tensor_scalar(acc_t[:, 0, n0:n1], acc_t[:, 0, n0:n1], TINY, None, ALU.max) \
                  .then_inc(den_done, 1)
            for c, ch in enumerate(CHUNKS):
                n0, n1 = ch[0] * NP_, (ch[-1] + 1) * NP_
                a0, a1 = ch[0], ch[-1] + 1
                dve.wait_ge(den_done, c + 1)
                nc.vector.reciprocal(acc_t[:, 0, n0:n1], acc_t[:, 0, n0:n1]).then_inc(rec_done, 1)
                dve.wait_ge(rec_done, c + 1)
                nc.vector.tensor_tensor(acc_t[:, 1, n0:n1], acc_t[:, 1, n0:n1], acc_t[:, 0, n0:n1], ALU.mult) \
                  .then_inc(agg_done, 1)

            dve.wait_ge(w_loaded, 16 * 3)
            for c, ch in enumerate(CHUNKS):
                a0, a1 = ch[0], ch[-1] + 1
                dve.wait_ge(mlp_done, c + 1)
                t = tmp[:, c % 2, 0:a1 - a0, :]
                nc.vector.scalar_tensor_tensor(
                    out=t, in0=ps_mt[0:NP_, c % 2, 0:(a1 - a0) * D].rearrange("p (a c) -> p a c", c=D),
                    scalar=0.0, in1=scale_bc[0:NP_, :].rearrange("p (a c) -> p a c", a=1)
                    .to_broadcast([NP_, a1 - a0, D]), op0=ALU.max, op1=ALU.mult).then_inc(relu_done, 1)
                dve.wait_ge(relu_done, c + 1)
                nc.vector.tensor_tensor(rs[:, a0:a1, :], t, rs[:, a0:a1, :], ALU.add).then_inc(out_done, 1)


_INS = ['x', 'src', 'dst', 'edge_attr_128', 'edge_weight', 'L1_gnn_mlp_w', 'L1_gnn_mlp_b', 'L1_gnn_scale']
_OUTS = [((3125, 128), 'float32')]


def kernel(**inputs):
    import numpy as _np
    import concourse.bacc as _bacc
    from concourse import mybir as _mybir
    from concourse.bass_utils import run_bass_kernel_spmd as _run

    nc = _bacc.Bacc("TRN2", target_bir_lowering=False, num_devices=1)
    arrays, args = {}, []
    for name in _INS:
        a = _np.ascontiguousarray(inputs[name])
        arrays[f"in_{name}_dram"] = a
        args.append(nc.dram_tensor(f"in_{name}_dram", a.shape, _mybir.dt.from_np(a.dtype),
                                   kind="ExternalInput").ap())
    for i, (shape, dtype) in enumerate(_OUTS):
        dt = _mybir.dt.from_np(_np.dtype(dtype))
        args.append(nc.dram_tensor(f"out_{i}_dram", shape, dt, kind="ExternalOutput").ap())
    gnn_kernel(nc, *args)
    r = _run(nc, [arrays], core_ids=[0])
    return r.results[0]["out_0_dram"]
```

```python
from contextlib import ExitStack

import concourse.bass as bass
from concourse import mybir

F32 = mybir.dt.float32
BF16 = mybir.dt.bfloat16
I32 = mybir.dt.int32
ALU = mybir.AluOpType
ACT = mybir.ActivationFunctionType

P = 128
LANES = 4
GROUP = P * LANES
SLOTS = 8
WINDOW = 64
AHEAD = 4
CHUNK = 4
EPS = 1e-5
BIG = 1.7e38
TINY = 1e-18


def gnn_kernel(nc, x, src, dst, edge_attr, edge_weight, mlp_w, mlp_b, scale, out):
    N, D = x.shape
    E = src.shape[0]
    NBLK = 25
    NP_ = N // NBLK
    assert NP_ * NBLK == N and NP_ <= P and D == P
    G = -(-E // GROUP)
    assert G % SLOTS == 0 and G <= P
    FULL = E // GROUP
    REST = E - FULL * GROUP
    RESTP, RESTJ = REST // LANES, REST % LANES
    assert FULL == G - 1 and REST > 0
    COLS = N + WINDOW
    CHUNKS = [list(range(a, min(a + CHUNK, NBLK))) for a in range(0, NBLK, CHUNK)]
    NCH = len(CHUNKS)

    h_table = nc.dram_tensor("h_table", [N + WINDOW, D], F32, kind="Internal").ap()
    side_tables = [nc.dram_tensor(f"side_table{j}", [N + P, D], F32, kind="Internal").ap()
                   for j in range(LANES)]
    h2_table = nc.dram_tensor("h2_table", [N, D], F32, kind="Internal").ap()

    def blocks(t):
        return t.rearrange("(a p) c -> p a c", p=NP_)

    with ExitStack() as ctx:
        def sb(name, shape, dt=F32):
            return ctx.enter_context(nc.sbuf_tensor(name, shape, dt))

        def psum(name, shape, dt=F32):
            return ctx.enter_context(nc.psum_tensor(name, shape, dt))

        def sem(name):
            return ctx.enter_context(nc.semaphore(name))

        ident = sb("ident", [P, P])
        identb = sb("identb", [P, P], BF16)
        iota_w = sb("iota_w", [P, WINDOW])
        below = sb("below", [P, P])
        spare = sb("spare", [P, 1])
        ones_row = sb("ones_row", [1, P])
        eps_col = sb("eps_col", [P, 1])
        tiny_col = sb("tiny_col", [P, 1])
        src_g = sb("src_g", [G, GROUP], I32)
        dst_g = sb("dst_g", [G, GROUP], I32)
        prev_g = sb("prev_g", [G, GROUP], I32)
        w_g = sb("w_g", [G, GROUP])
        src_f = sb("src_f", [G, GROUP])
        dst_f = sb("dst_f", [G, GROUP])
        rel_f = sb("rel_f", [G, GROUP])
        same_f = sb("same_f", [G, GROUP])
        cap_g = sb("cap_g", [G, GROUP], BF16)
        lo_i = sb("lo_i", [G, GROUP], I32)
        hi_i = sb("hi_i", [G, GROUP], I32)
        lo_g = sb("lo_g", [G, GROUP], BF16)
        hi_g = sb("hi_g", [G, GROUP], BF16)
        idx_t = sb("idx_t", [P, G + SLOTS, LANES])
        rel_t = sb("rel_t", [P, G, LANES])
        w_t = sb("w_t", [P, G, LANES])
        to_spare = sb("to_spare", [P, G, LANES])
        base_row = sb("base_row", [1, G], I32)
        idx0 = sb("idx0", [P, SLOTS, LANES], I32)
        idx1 = sb("idx1", [P, SLOTS, LANES], I32)
        xs = sb("xs", [NP_, NBLK, D])
        hs = sb("hs", [NP_, NBLK, D])
        rs = sb("rs", [NP_, NBLK, D])
        stats = sb("stats", [NP_, NBLK, 6])
        meanvar = sb("meanvar", [NP_, NBLK, 2])
        std = sb("std", [NP_, NBLK])
        rstd = sb("rstd", [NP_, NBLK])
        shift = sb("shift", [NP_, NBLK])
        acc_t = sb("acc_t", [P, 2, COLS])
        hwin = sb("hwin", [WINDOW, SLOTS, D])
        msg = sb("msg", [P, SLOTS, LANES, D])
        equal = sb("equal", [P, 2, LANES, P])
        earlier = sb("earlier", [P, LANES, P])
        count = sb("count", [P, 2, LANES])
        away = sb("away", [P, 2, LANES])
        oh0 = sb("oh0", [P, 2, LANES, WINDOW])
        ohw = sb("ohw", [P, 2, LANES, WINDOW])
        mix = sb("mix", [WINDOW, 2, LANES, P])
        side_in = sb("side_in", [NP_, 2, LANES, CHUNK, D])
        pair = sb("pair", [NP_, 2, LANES // 2, CHUNK, D])
        m = sb("m", [P, SLOTS, LANES, D])
        mt = sb("mt", [P, 2, GROUP])
        mx = sb("mx", [P, 4, GROUP])
        ec = sb("ec", [P, 2, 2, LANES, D])
        oh = sb("oh", [P, 2, LANES, WINDOW])
        drop = sb("drop", [P, 4])
        fac = sb("fac", [P, 4])
        guess = m[:, :, :, :].rearrange("p s j c -> p (s j c)")[:, 0:N]
        w_sb = sb("w_sb", [D, D])
        w_tr = sb("w_tr", [D, D])
        b_row = sb("b_row", [1, D])
        scale_bc = sb("scale_bc", [P, D])
        tmp = sb("tmp", [NP_, 2, CHUNK, D])

        ps_mt = psum("ps_mt", [P, 2, GROUP])
        ps_cap = psum("ps_cap", [P, 2, GROUP])
        ps_b = psum("ps_b", [P, 2, LANES, D])
        ps_sum = psum("ps_sum", [P, 2, GROUP])

        x_loaded = [sem(f"x_loaded{c}") for c in range(NCH)]
        lists_set = sem("lists_set")
        lists_loaded = sem("lists_loaded")
        w_loaded = sem("w_loaded")
        idents_zero = sem("idents_zero")
        idents_ready = sem("idents_ready")
        below_ones = sem("below_ones")
        window_cols = sem("window_cols")
        spares_ready = sem("spares_ready")
        ones_ready = sem("ones_ready")
        eps_ready = sem("eps_ready")
        acc_zero = sem("acc_zero")
        stats_done = sem("stats_done")
        aggr_done = sem("aggr_done")
        std_done = sem("std_done")
        rstd_done = sem("rstd_done")
        shift_done = sem("shift_done")
        h_raw = sem("h_raw")
        h_last = sem("h_last")
        h_done = sem("h_done")
        xh_done = sem("xh_done")
        h_written = sem("h_written")
        src_real = sem("src_real")
        dst_real = sem("dst_real")
        rel_done = sem("rel_done")
        digits_split = sem("digits_split")
        digits_ready = sem("digits_ready")
        same_done = sem("same_done")
        caps_ready = sem("caps_ready")
        src_turned = sem("src_turned")
        rel_turned = sem("rel_turned")
        w_turned = sem("w_turned")
        base_turned = sem("base_turned")
        mlp_turned = sem("mlp_turned")
        idx_ready = sem("idx_ready")
        rel_ready = sem("rel_ready")
        weights_ready = sem("weights_ready")
        base_ready = sem("base_ready")
        spare_ready = sem("spare_ready")
        mlp_ready = sem("mlp_ready")
        scatter_open = sem("scatter_open")
        gather_open = sem("gather_open")
        zeroed = sem("zeroed")
        pad_cleared = sem("pad_cleared")
        side_cleared = [sem(f"side_cleared{j}") for j in range(LANES)]
        win_loaded = [sem(f"win_loaded{s}") for s in range(SLOTS)]
        src_spread = sem("src_spread")
        equal_done = sem("equal_done")
        oh0_done = sem("oh0_done")
        ohw_done = sem("ohw_done")
        count_done = sem("count_done")
        away_done = sem("away_done")
        idx0_ready = sem("idx0_ready")
        mix_summed = sem("mix_summed")
        mix_done = sem("mix_done")
        msg_summed = sem("msg_summed")
        msg_ready = sem("msg_ready")
        scattered = [sem(f"scattered{j}") for j in range(LANES)]
        side_loaded = [sem(f"side_loaded{c}") for c in range(NCH)]
        pairs_done = sem("pairs_done")
        half_done = sem("half_done")
        x1_done = sem("x1_done")
        stats1_done = sem("stats1_done")
        aggr1_done = sem("aggr1_done")
        std1_done = sem("std1_done")
        rstd1_done = sem("rstd1_done")
        shift1_done = sem("shift1_done")
        h2_raw = sem("h2_raw")
        h2_last = sem("h2_last")
        h2_done = sem("h2_done")
        r_done = sem("r_done")
        h2_written = sem("h2_written")
        idx1_ready = sem("idx1_ready")
        ea_loaded = [sem(f"ea_loaded{s}") for s in range(SLOTS)]
        rest_loaded = sem("rest_loaded")
        m_ready = [sem(f"m_ready{s}") for s in range(SLOTS)]
        mt_done = sem("mt_done")
        evac_done = sem("evac_done")
        scan_done = sem("scan_done")
        rev_done = sem("rev_done")
        drop_done = sem("drop_done")
        fac_done = sem("fac_done")
        b_done = sem("b_done")
        sub_done = sem("sub_done")
        exp_done = sem("exp_done")
        mul_done = sem("mul_done")
        oh_done = sem("oh_done")
        sums_done = sem("sums_done")
        rescaled = sem("rescaled")
        added = sem("added")
        ln_done = sem("ln_done")
        guess_done = sem("guess_done")
        quot_done = sem("quot_done")
        check_done = sem("check_done")
        agg_done = sem("agg_done")
        mlp_done = sem("mlp_done")
        relu_done = sem("relu_done")
        out_done = sem("out_done")
        out_written = sem("out_written")

        block = ctx.enter_context(nc.Block())

        def pipeline(eng, step, lag, peel=1):
            for n in range(SLOTS * peel):
                step(n // SLOTS, n % SLOTS, lambda d, n=n: n - d >= 0)
            with eng.Fori(peel, G // SLOTS) as i:
                for k in range(SLOTS):
                    step(i, k, lambda d: d <= SLOTS * peel)
            for k in range(lag):
                step(G // SLOTS, k, lambda d, k=k: d > k)

        def mlp_bank(c):
            if c % 4 < 2:
                return ps_mt[0:NP_, c % 2, :]
            return ps_cap[0:NP_, c % 2, :]

        def use(i, k, d=0):
            return i if k >= d else i - 1

        def group(i, k, d=0):
            return i * SLOTS + (k - d)

        @block.sync
        def _(sp):
            for c, ch in enumerate(CHUNKS):
                sp.dma_start(xs[:, ch[0]:ch[-1] + 1, :],
                             blocks(x)[:, ch[0]:ch[-1] + 1, :]).then_inc(x_loaded[c], 16)
            sp.wait_ge(zeroed, 1)
            sp.dma_start(h_table[N:N + WINDOW, :], rs[0:WINDOW, 0, :]).then_inc(pad_cleared, 16)

            def clear_side(j):
                t = side_tables[j]
                sp.dma_start(blocks(t[0:N, :]), rs[:, :, :]).then_inc(side_cleared[j], 16)
                sp.dma_start(t[N:N + P, :].rearrange("(p a) c -> p a c", a=2), rs[0:P // 2, 0:2, :]) \
                  .then_inc(side_cleared[j], 16)

            clear_side(0)
            clear_side(1)
            for c, ch in enumerate(CHUNKS):
                sp.wait_ge(h_done, ch[-1] - c)
                sp.wait_ge(h_last, c + 1)
                sp.dma_start(blocks(h_table[0:N, :])[:, ch[0]:ch[-1] + 1, :],
                             hs[:, ch[0]:ch[-1] + 1, :]).then_inc(h_written, 16)

            clear_side(2)
            clear_side(3)

            def load_group(slot, rows):
                sp.dma_start(m[:, slot, :, :], rows.rearrange("(p j) c -> p j c", j=LANES)) \
                  .then_inc(ea_loaded[slot], 16)

            sp.wait_ge(h_written, 16 * NCH)
            sp.wait_ge(pad_cleared, 16)
            sp.wait_ge(base_ready, 1)

            def load_window(i, k, live):
                g = group(i, k)
                if live(SLOTS):
                    sp.wait_ge(msg_summed, g - SLOTS + 1)
                start = sp.value_load(base_row[0:1, bass.ds(g, 1)], min_val=0, max_val=N - 1)
                sp.dma_start(hwin[:, k, :], h_table[bass.ds(start, WINDOW), :]).then_inc(win_loaded[k], 16)
                if not live(SLOTS) and k == SLOTS - 1:
                    for s in range(SLOTS):
                        load_group(s, edge_attr[s * GROUP:(s + 1) * GROUP, :])

            pipeline(sp, load_window, 0)

            for j in range(LANES):
                sp.wait_ge(scattered[j], 16 * G)
            for c, ch in enumerate(CHUNKS):
                if c >= 2:
                    sp.wait_ge(pairs_done, c - 1)
                for j, t in enumerate(side_tables):
                    sp.dma_start(side_in[:, c % 2, j, 0:len(ch), :],
                                 blocks(t[0:N, :])[:, ch[0]:ch[-1] + 1, :]).then_inc(side_loaded[c], 16)
            for c, ch in enumerate(CHUNKS):
                sp.wait_ge(h2_done, ch[-1] - c)
                sp.wait_ge(h2_last, c + 1)
                sp.dma_start(blocks(h2_table)[:, ch[0]:ch[-1] + 1, :],
                             hs[:, ch[0]:ch[-1] + 1, :]).then_inc(h2_written, 16)
            with sp.Fori(1, G // SLOTS - 1) as i:
                for k in range(SLOTS):
                    sp.wait_ge(mul_done, (i - 1) * SLOTS + k + 1)
                    load_group(k, edge_attr[bass.ds((i * SLOTS + k) * GROUP, GROUP), :])
            for k in range(SLOTS):
                g = G - SLOTS + k
                sp.wait_ge(mul_done, g - SLOTS + 1)
                if g < FULL:
                    load_group(k, edge_attr[g * GROUP:(g + 1) * GROUP, :])
                else:
                    rows = edge_attr[g * GROUP:g * GROUP + RESTP * LANES, :]
                    sp.dma_start(m[0:RESTP, k, :, :], rows.rearrange("(p j) c -> p j c", j=LANES)) \
                      .then_inc(ea_loaded[k], 16)
                    sp.dma_start(m[RESTP:RESTP + 1, k, 0:RESTJ, :],
                                 edge_attr[E - RESTJ:E, :].rearrange("(p j) c -> p j c", j=RESTJ)) \
                      .then_inc(rest_loaded, 16)
            for c, ch in enumerate(CHUNKS):
                sp.wait_ge(out_done, c + 1)
                sp.dma_start(blocks(out)[:, ch[0]:ch[-1] + 1, :],
                             rs[:, ch[0]:ch[-1] + 1, :]).then_inc(out_written, 16)
            sp.wait_ge(out_written, 16 * NCH)

        @block.gpsimd
        def _(pool):
            nc.gpsimd.memset(dst_g[:, :], -1).then_inc(lists_set, 1)
            nc.gpsimd.memset(prev_g[:, :], -1).then_inc(lists_set, 1)
            nc.gpsimd.memset(src_g[:, :], 0).then_inc(lists_set, 1)
            nc.gpsimd.memset(w_g[:, :], 0.0).then_inc(lists_set, 1)
            nc.gpsimd.memset(ident[:, :], 0.0).then_inc(idents_zero, 1)
            nc.gpsimd.memset(identb[:, :], 0.0).then_inc(idents_zero, 1)
            nc.gpsimd.memset(below[:, :], 1.0).then_inc(below_ones, 1)
            pool.wait_ge(idents_zero, 2)
            for t in (ident, identb):
                nc.gpsimd.affine_select(out=t[:, :], in_=t[:, :], compare_op=ALU.not_equal, fill=1.0, base=0,
                                        pattern=[[-1, P]], channel_multiplier=1).then_inc(idents_ready, 1)
            pool.wait_ge(below_ones, 1)
            nc.gpsimd.affine_select(out=below[:, :], in_=below[:, :], compare_op=ALU.is_gt, fill=0.0, base=0,
                                    pattern=[[-1, P]], channel_multiplier=1).then_inc(window_cols, 1)
            nc.gpsimd.iota(iota_w[:, :], pattern=[[1, WINDOW]], base=0, channel_multiplier=0,
                           allow_small_or_imprecise_dtypes=True).then_inc(window_cols, 1)
            nc.gpsimd.iota(spare[:, :], pattern=[[1, 1]], base=N, channel_multiplier=1,
                           allow_small_or_imprecise_dtypes=True).then_inc(window_cols, 1)
            nc.gpsimd.memset(ones_row[:, :], 1.0).then_inc(ones_ready, 1)
            nc.gpsimd.memset(idx_t[:, G:G + SLOTS, :], 0.0).then_inc(spares_ready, 1)

            def scatter0(i, k, live):
                pool.wait_ge(msg_ready, group(i, k) + 1)
                pool.wait_ge(idx0_ready, group(i, k) + 1)
                for j in range(LANES):
                    if live(1):
                        pool.wait_ge(scattered[j], group(i, k) * 16)
                    else:
                        pool.wait_ge(side_cleared[j], 32)
                    pool.sem_inc(scatter_open, 1)
                    nc.gpsimd.indirect_dma_start(
                        side_tables[j][:, :], bass.IndirectOffsetOnAxis(ap=idx0[:, k, j:j + 1], axis=0),
                        msg[:, k, j, :], None, compute_op=ALU.add).then_inc(scattered[j], 16)

            pipeline(pool, scatter0, 0)

            for c, ch in enumerate(CHUNKS):
                n = len(ch)
                pool.wait_ge(side_loaded[c], 16 * LANES)
                if c >= 2:
                    pool.wait_ge(x1_done, c - 1)
                nc.gpsimd.tensor_tensor(pair[:, c % 2, :, 0:n, :], side_in[:, c % 2, 0::2, 0:n, :],
                                        side_in[:, c % 2, 1::2, 0:n, :], ALU.add).then_inc(pairs_done, 1)
            pool.wait_ge(h2_written, 16 * NCH)

            def gather1(i, k, live):
                pool.wait_ge(idx1_ready, group(i, k) + 1)
                pool.wait_ge(ea_loaded[k], (i + 1) * 16)
                pool.sem_inc(gather_open, 1)
                for j in range(LANES):
                    nc.gpsimd.indirect_dma_start(
                        m[:, k, j, :], None, h2_table[:, :],
                        bass.IndirectOffsetOnAxis(ap=idx1[:, k, j:j + 1], axis=0),
                        compute_op=ALU.add).then_inc(m_ready[k], 16)

            pipeline_last = G // SLOTS - 1
            for k in range(SLOTS):
                gather1(0, k, None)
            with pool.Fori(1, pipeline_last) as i:
                for k in range(SLOTS):
                    gather1(i, k, None)
            for k in range(SLOTS):
                if k == SLOTS - 1:
                    pool.wait_ge(rest_loaded, 16)
                gather1(pipeline_last, k, None)

            for c, ch in enumerate(CHUNKS):
                cols = acc_t[:, 1, ch[0] * NP_:(ch[-1] + 1) * NP_]
                pool.wait_ge(guess_done, c + 1)
                nc.gpsimd.tensor_tensor(cols, cols, guess[:, ch[0] * NP_:(ch[-1] + 1) * NP_], ALU.mult) \
                  .then_inc(quot_done, 1)

        @block.scalar
        def _(act):
            act.wait_ge(lists_set, 4)
            for t, v in ((dst_g, dst), (src_g, src), (w_g, edge_weight)):
                act.dma_start(t[0:FULL, :], v[0:FULL * GROUP].rearrange("(g e) -> g e", e=GROUP)) \
                   .then_inc(lists_loaded, 16)
                act.dma_start(t[FULL:G, 0:REST], v[FULL * GROUP:E].rearrange("(g e) -> g e", g=1)) \
                   .then_inc(lists_loaded, 16)
            act.dma_start(prev_g[0:1, 1:GROUP], dst[0:GROUP - 1].rearrange("(g e) -> g e", g=1)) \
               .then_inc(lists_loaded, 16)
            act.dma_start(prev_g[1:FULL, :],
                          dst[GROUP - 1:FULL * GROUP - 1].rearrange("(g e) -> g e", e=GROUP)) \
               .then_inc(lists_loaded, 16)
            act.dma_start(prev_g[FULL:G, 0:REST + 1], dst[FULL * GROUP - 1:E].rearrange("(g e) -> g e", g=1)) \
               .then_inc(lists_loaded, 16)

            def normalize(stat_sem, std_sem, shift_sem, done):
                for c, ch in enumerate(CHUNKS):
                    a0, a1 = ch[0], ch[-1] + 1
                    act.wait_ge(stat_sem, a1)
                    nc.scalar.activation(std[:, a0:a1], meanvar[:, a0:a1, 1], ACT.Sqrt,
                                         bias=eps_col[0:NP_, 0:1]).then_inc(std_sem, 1)
                    act.wait_ge(shift_sem, c + 1)
                    for a in ch[:-1]:
                        nc.scalar.activation(hs[:, a, :], xs[:, a, :], ACT.Relu, bias=shift[:, a:a + 1],
                                             scale=rstd[:, a:a + 1]).then_inc(done, 1)

            act.wait_ge(eps_ready, 2)
            normalize(aggr_done, std_done, shift_done, h_done)

            act.dma_start(w_sb[:, :], mlp_w).then_inc(w_loaded, 16)
            act.dma_start(b_row[:, :], mlp_b.rearrange("(a n) -> a n", a=1)).then_inc(w_loaded, 16)
            act.dma_start(scale_bc[:, :], scale.rearrange("(a n) -> a n", a=1).to_broadcast([P, D])) \
               .then_inc(w_loaded, 16)

            def mix_and_messages(i, k, live):
                if live(1):
                    g, b = group(i, k, 1), (k - 1) % 2
                    pe_done = mix_summed
                    act.wait_ge(pe_done, g + 1)
                    if live(3):
                        act.wait_ge(msg_summed, g - 1)
                    nc.scalar.copy(mix[:, b, :, :], ps_mt[0:WINDOW, b, :].rearrange("d (j e) -> d j e", j=LANES)) \
                      .then_inc(mix_done, 1)
                if live(2):
                    g, b = group(i, k, 2), k % 2
                    act.wait_ge(msg_summed, g + 1)
                    if live(2 + SLOTS):
                        for j in range(LANES):
                            act.wait_ge(scattered[j], (g - SLOTS + 1) * 16)
                    nc.scalar.copy(msg[:, (k - 2) % SLOTS, :, :], ps_b[:, b, :, :]).then_inc(msg_ready, 1)

            pipeline(act, mix_and_messages, 2, peel=2)

            act.wait_ge(idx_ready, 1)
            act.wait_ge(spares_ready, 1)
            for s in range(AHEAD):
                nc.scalar.copy(idx1[:, s, :], idx_t[:, s, :]).then_inc(idx1_ready, 1)
            act.wait_ge(h_written, 16 * NCH)
            normalize(aggr1_done, std1_done, shift1_done, h2_done)

            def stage(i, k, live):
                s = (k + AHEAD) % SLOTS
                if live(SLOTS - AHEAD):
                    act.wait_ge(m_ready[s], (use(i, k, SLOTS - AHEAD) + 1) * 16 * LANES)
                nc.scalar.copy(idx1[:, s, :], idx_t[:, bass.ds(group(i, k) + AHEAD, 1), :]
                               .rearrange("p a j -> p (a j)")).then_inc(idx1_ready, 1)

            def step(i, k, live):
                if live(2):
                    g = group(i, k, 2)
                    act.wait_ge(sub_done, g + 1)
                    e = ec[:, k % 2, 0, :, :]
                    nc.scalar.activation(e, e, ACT.Exp).then_inc(exp_done, 1)
                if live(0):
                    g = group(i, k)
                    act.wait_ge(mt_done, g + 1)
                    if live(2):
                        act.wait_ge(scan_done, g - 1)
                    nc.scalar.copy(mt[:, k % 2, :], ps_mt[:, k % 2, :]).then_inc(evac_done, 1)
                    stage(i, k, live)
                if live(1):
                    g, c = group(i, k, 1), (k - 1) % 4
                    act.wait_ge(drop_done, g + 1)
                    if live(5):
                        act.wait_ge(added, g - 3)
                    nc.scalar.activation(fac[:, c:c + 1], drop[:, c:c + 1], ACT.Exp).then_inc(fac_done, 1)

            pipeline(act, step, 2)

            act.wait_ge(added, G)
            for c, ch in enumerate(CHUNKS):
                n0, n1 = ch[0] * NP_, (ch[-1] + 1) * NP_
                nc.scalar.activation(guess[:, n0:n1], acc_t[:, 0, n0:n1], ACT.Ln, bias=tiny_col[:, 0:1]) \
                  .then_inc(ln_done, 1)
            for c, ch in enumerate(CHUNKS):
                n0, n1 = ch[0] * NP_, (ch[-1] + 1) * NP_
                act.wait_ge(ln_done, c + 1)
                nc.scalar.activation(guess[:, n0:n1], guess[:, n0:n1], ACT.Exp, scale=-1.0) \
                  .then_inc(guess_done, 1)

        @block.tensor
        def _(pe):
            pe.wait_ge(idents_ready, 2)
            for t, bank, loaded, count_, done in (
                    (src_f, ps_mt[:, 0, :], src_real, 1, src_turned), (rel_f, ps_mt[:, 1, :], rel_done, 1, rel_turned),
                    (w_g, ps_cap[:, 0, :], lists_loaded, 16 * 9, w_turned)):
                pe.wait_ge(loaded, count_)
                for j in range(LANES):
                    mm = pe.transpose(bank[:, j * G:(j + 1) * G], t[:, j::LANES], ident[0:G, 0:G])
                mm.then_inc(done, 1)
            pe.transpose(ps_cap[0:1, 1, 0:G], dst_f[:, 0:1], ident[0:G, 0:G]).then_inc(base_turned, 1)
            pe.wait_ge(w_loaded, 16 * 3)
            pe.transpose(ps_sum[:, 0, 0:D], w_sb[:, :], ident[:, :]).then_inc(mlp_turned, 1)

            pe.wait_ge(digits_ready, 2)
            pe.wait_ge(idx_ready, 1)
            pe.wait_ge(rel_ready, 1)
            pe.wait_ge(weights_ready, 1)
            pe.wait_ge(base_ready, 1)

            def messages(i, k, live):
                if live(0):
                    g, b = group(i, k), k % 2
                    if live(2):
                        pe.wait_ge(equal_done, g - 1)
                    pick = identb[0:G, bass.ds(g, 1)].to_broadcast([G, P])
                    pe.matmul(ps_cap[:, b, :], pick, hi_g[:, :], start=True, stop=False)
                    pe.matmul(ps_cap[:, b, :], pick, lo_g[:, :], start=False, stop=True) \
                      .then_inc(src_spread, 1)
                if live(1):
                    g, b = group(i, k, 1), (k - 1) % 2
                    pe.wait_ge(equal_done, g + 1)
                    pe.wait_ge(ohw_done, g + 1)
                    if live(3):
                        pe.wait_ge(mix_done, g - 1)
                    for j in range(LANES):
                        mm = pe.matmul(ps_mt[0:WINDOW, b, j * P:(j + 1) * P], ohw[:, b, j, :],
                                       equal[:, b, j, :], start=True, stop=True)
                    mm.then_inc(mix_summed, 1)
                if live(2):
                    g, b = group(i, k, 2), k % 2
                    pe.wait_ge(mix_done, g + 1)
                    pe.wait_ge(win_loaded[(k - 2) % SLOTS], (use(i, k, 2) + 1) * 16)
                    if live(4):
                        pe.wait_ge(msg_ready, g - 1)
                    for j in range(LANES):
                        mm = pe.matmul(ps_b[:, b, j, :], mix[:, b, j, :], hwin[:, (k - 2) % SLOTS, :],
                                       start=True, stop=True)
                    mm.then_inc(msg_summed, 1)

            pipeline(pe, messages, 2)
            pe.wait_ge(msg_ready, G)
            pe.wait_ge(mlp_ready, 1)
            pe.wait_ge(caps_ready, 1)

            def step(i, k, live):
                if live(0):
                    g, b = group(i, k), k % 2
                    pe.wait_ge(m_ready[k], (i + 1) * 16 * LANES)
                    if live(2):
                        pe.wait_ge(evac_done, g - 1)
                    if live(2):
                        pe.wait_ge(rev_done, g - 1)
                    for j in range(LANES):
                        pe.transpose(ps_mt[:, b, j::LANES], m[:, k, j, :], ident[:, :])
                    pick = identb[0:G, bass.ds(g, 1)].to_broadcast([G, P])
                    pe.matmul(ps_cap[:, b, :], pick, cap_g[:, :], start=True, stop=True) \
                      .then_inc(mt_done, 1)
                if live(1):
                    g, b = group(i, k, 1), (k - 1) % 2
                    pe.wait_ge(rev_done, g + 1)
                    if live(3):
                        pe.wait_ge(sub_done, g - 1)
                    for j in range(LANES):
                        mm = pe.transpose(ps_b[:, b, j, :], mx[:, (k - 1) % 4, j::LANES], ident[:, :])
                    mm.then_inc(b_done, 1)
                if live(2):
                    g, b = group(i, k, 2), k % 2
                    pe.wait_ge(mul_done, g + 1)
                    pe.wait_ge(oh_done, g + 1)
                    if live(4):
                        pe.wait_ge(added, g - 1)
                    for q in range(2):
                        for j in range(LANES):
                            mm = pe.matmul(ps_sum[:, b, q * WINDOW:(q + 1) * WINDOW], ec[:, b, q, j, :],
                                           oh[:, b, j, :], start=(j == 0), stop=(j == LANES - 1))
                    mm.then_inc(sums_done, 1)

            pipeline(pe, step, 2)

            pe.wait_ge(ones_ready, 1)
            for c, ch in enumerate(CHUNKS):
                pe.wait_ge(agg_done, c + 1)
                if c >= 4:
                    pe.wait_ge(relu_done, c - 3)
                for q, a in enumerate(ch):
                    o = mlp_bank(c)[:, q * D:(q + 1) * D]
                    pe.matmul(o, acc_t[:, 1, a * NP_:(a + 1) * NP_], w_tr[:, :], start=True, stop=False)
                    mm = pe.matmul(o, ones_row[:, 0:NP_], b_row[:, :], start=False, stop=True)
                mm.then_inc(mlp_done, 1)

        @block.vector
        def _(dve):
            nc.vector.memset(eps_col[:, :], EPS).then_inc(eps_ready, 1)
            nc.vector.memset(tiny_col[:, :], TINY).then_inc(eps_ready, 1)
            nc.vector.memset(rs[:, :, :], 0.0).then_inc(zeroed, 1)

            def norm_stats(c, ch, stats_sem, aggr_sem):
                for a in ch:
                    nc.vector.bn_stats(stats[:, a, :], xs[:, a, :]).then_inc(stats_sem, 1)
                dve.wait_ge(stats_sem, ch[-1] + 1)
                for a in ch:
                    nc.vector.bn_aggr(meanvar[:, a, :], stats[:, a, :]).then_inc(aggr_sem, 1)

            def norm_scale(c, ch, std_sem, rstd_sem, shift_sem, raw_sem, last_sem):
                a0, a1 = ch[0], ch[-1] + 1
                dve.wait_ge(std_sem, c + 1)
                nc.vector.reciprocal(rstd[:, a0:a1], std[:, a0:a1]).then_inc(rstd_sem, 1)
                dve.wait_ge(rstd_sem, c + 1)
                nc.vector.scalar_tensor_tensor(out=shift[:, a0:a1], in0=meanvar[:, a0:a1, 0], scalar=-1.0,
                                               in1=rstd[:, a0:a1], op0=ALU.mult, op1=ALU.mult) \
                  .then_inc(shift_sem, 1)
                dve.wait_ge(shift_sem, c + 1)
                a = ch[-1]
                nc.vector.tensor_scalar(hs[:, a, :], xs[:, a, :], rstd[:, a:a + 1], shift[:, a:a + 1],
                                        ALU.mult, ALU.add).then_inc(raw_sem, 1)
                dve.wait_ge(raw_sem, c + 1)
                nc.vector.tensor_scalar(hs[:, a, :], hs[:, a, :], 0.0, None, ALU.max).then_inc(last_sem, 1)

            for c, ch in enumerate(CHUNKS):
                dve.wait_ge(x_loaded[c], 16)
                norm_stats(c, ch, stats_done, aggr_done)
                if c >= 1:
                    norm_scale(c - 1, CHUNKS[c - 1], std_done, rstd_done, shift_done, h_raw, h_last)
            norm_scale(NCH - 1, CHUNKS[-1], std_done, rstd_done, shift_done, h_raw, h_last)

            dve.wait_ge(lists_loaded, 16 * 9)
            nc.vector.tensor_copy(dst_f[:, :], dst_g[:, :]).then_inc(dst_real, 1)
            nc.vector.tensor_copy(src_f[:, :], src_g[:, :]).then_inc(src_real, 1)
            dve.wait_ge(dst_real, 1)
            nc.vector.tensor_scalar(rel_f[:, :], dst_f[:, :], dst_f[:, 0:1], None, ALU.subtract) \
              .then_inc(rel_done, 1)
            nc.vector.tensor_scalar(lo_i[:, :], src_g[:, :], WINDOW - 1, None, ALU.bitwise_and) \
              .then_inc(digits_split, 1)
            nc.vector.tensor_scalar(hi_i[:, :], src_g[:, :], -WINDOW, None, ALU.bitwise_and) \
              .then_inc(digits_split, 1)
            dve.wait_ge(digits_split, 1)
            nc.vector.tensor_copy(lo_g[:, :], lo_i[:, :]).then_inc(digits_ready, 1)
            dve.wait_ge(digits_split, 2)
            nc.vector.tensor_copy(hi_g[:, :], hi_i[:, :]).then_inc(digits_ready, 1)

            def turned(bank):
                return bank[:, 0:LANES * G].rearrange("p (j g) -> p g j", j=LANES)

            dve.wait_ge(src_turned, 1)
            nc.vector.tensor_copy(idx_t[:, 0:G, :], turned(ps_mt[:, 0, :])).then_inc(idx_ready, 1)
            dve.wait_ge(rel_turned, 1)
            nc.vector.tensor_copy(rel_t[:, :, :], turned(ps_mt[:, 1, :])).then_inc(rel_ready, 1)
            dve.wait_ge(w_turned, 1)
            nc.vector.tensor_copy(w_t[:, :, :], turned(ps_cap[:, 0, :])).then_inc(weights_ready, 1)
            dve.wait_ge(base_turned, 1)
            nc.vector.tensor_copy(base_row[:, :], ps_cap[0:1, 1, 0:G]).then_inc(base_ready, 1)
            dve.wait_ge(window_cols, 3)
            dve.wait_ge(idx_ready, 1)
            nc.vector.tensor_scalar(to_spare[:, :, :], idx_t[:, 0:G, :], -1.0, spare[:, 0:1], ALU.mult, ALU.add) \
              .then_inc(spare_ready, 1)
            dve.wait_ge(rel_ready, 1)
            dve.wait_ge(weights_ready, 1)
            dve.wait_ge(spare_ready, 1)

            lanes = [P, LANES, WINDOW]

            def window_match(o, i, k, d, done):
                nc.vector.tensor_tensor(o, iota_w[:, :].rearrange("p (a w) -> p a w", a=1).to_broadcast(lanes),
                                        rel_t[:, bass.ds(group(i, k, d), 1), :]
                                        .rearrange("p a j -> p j a").to_broadcast(lanes),
                                        ALU.is_equal).then_inc(done, 1)

            def window_start(i, k, d):
                return dve.value_load(base_row[0:1, bass.ds(group(i, k, d), 1)], min_val=0, max_val=N - 1)

            def step0(i, k, live):
                g, b = group(i, k), k % 2
                dve.wait_ge(src_spread, g + 1)
                if live(2):
                    dve.wait_ge(mix_summed, g - 1)
                nc.vector.tensor_tensor(equal[:, b, :, :],
                                        ps_cap[:, b, :].rearrange("p (e j) -> p j e", j=LANES),
                                        idx_t[:, bass.ds(g, 1), :].rearrange("p a j -> p j a")
                                        .to_broadcast([P, LANES, P]), ALU.is_equal).then_inc(equal_done, 1)
                window_match(oh0[:, b, :, :], i, k, 0, oh0_done)
                dve.wait_ge(equal_done, g + 1)
                for j in range(LANES):
                    nc.vector.tensor_tensor_reduce(earlier[:, j, :], equal[:, b, j, :], below[:, :], 1.0, 0.0,
                                                   ALU.mult, ALU.add, count[:, b, j:j + 1]) \
                      .then_inc(count_done, 1)
                dve.wait_ge(oh0_done, g + 1)
                nc.vector.tensor_tensor(ohw[:, b, :, :], oh0[:, b, :, :],
                                        w_t[:, bass.ds(g, 1), :].rearrange("p a j -> p j a")
                                        .to_broadcast(lanes), ALU.mult).then_inc(ohw_done, 1)
                dve.wait_ge(count_done, (g + 1) * LANES)
                nc.vector.scalar_tensor_tensor(out=away[:, b, :], in0=count[:, b, :], scalar=1.0,
                                               in1=to_spare[:, bass.ds(g, 1), :].rearrange("p a j -> p (a j)"),
                                               op0=ALU.min, op1=ALU.mult).then_inc(away_done, 1)
                if live(SLOTS):
                    for j in range(LANES):
                        dve.wait_ge(scattered[j], (g - SLOTS + 1) * 16)
                dve.wait_ge(away_done, g + 1)
                nc.vector.tensor_tensor(idx0[:, k, :], away[:, b, :],
                                        idx_t[:, bass.ds(g, 1), :].rearrange("p a j -> p (a j)"),
                                        ALU.add).then_inc(idx0_ready, 1)

            pipeline(dve, step0, 0)

            dve.wait_ge(h_done, NBLK - NCH)
            dve.wait_ge(h_last, NCH)
            nc.vector.scalar_tensor_tensor(out=xs[:, :, :], in0=hs[:, :, :], scalar=0.25, in1=xs[:, :, :],
                                           op0=ALU.mult, op1=ALU.add).then_inc(xh_done, 1)
            nc.vector.tensor_tensor(same_f[:, :], dst_g[:, :], prev_g[:, :], ALU.is_equal).then_inc(same_done, 1)
            dve.wait_ge(same_done, 1)
            nc.vector.tensor_scalar(cap_g[:, :], same_f[:, :], 2 * BIG, -BIG, ALU.mult, ALU.add) \
              .then_inc(caps_ready, 1)
            dve.wait_ge(mlp_turned, 1)
            nc.vector.tensor_copy(w_tr[:, :], ps_sum[:, 0, 0:D]).then_inc(mlp_ready, 1)
            nc.vector.memset(acc_t[:, :, :], 0.0).then_inc(acc_zero, 1)
            dve.wait_ge(acc_zero, 1)
            dve.wait_ge(xh_done, 1)

            for c, ch in enumerate(CHUNKS):
                a0, a1 = ch[0], ch[-1] + 1
                n = a1 - a0
                dve.wait_ge(pairs_done, c + 1)
                for q, done in enumerate((half_done, x1_done)):
                    nc.vector.scalar_tensor_tensor(out=xs[:, a0:a1, :], in0=pair[:, c % 2, q, 0:n, :],
                                                   scalar=0.75, in1=xs[:, a0:a1, :], op0=ALU.mult,
                                                   op1=ALU.add).then_inc(done, 1)
                    dve.wait_ge(done, c + 1)
                norm_stats(c, ch, stats1_done, aggr1_done)
                if c >= 1:
                    norm_scale(c - 1, CHUNKS[c - 1], std1_done, rstd1_done, shift1_done, h2_raw, h2_last)
            norm_scale(NCH - 1, CHUNKS[-1], std1_done, rstd1_done, shift1_done, h2_raw, h2_last)
            dve.wait_ge(h2_done, NBLK - NCH)
            dve.wait_ge(h2_last, NCH)
            nc.vector.tensor_tensor(rs[:, :, :], xs[:, :, :], hs[:, :, :], ALU.add).then_inc(r_done, 1)

            def step(i, k, live):
                if live(2):
                    g, b = group(i, k, 2), k % 2
                    dve.wait_ge(b_done, g + 1)
                    if live(4):
                        dve.wait_ge(sums_done, g - 1)
                    nc.vector.tensor_tensor(ec[:, b, 0, :, :], m[:, (k - 2) % SLOTS, :, :], ps_b[:, b, :, :],
                                            ALU.subtract).then_inc(sub_done, 1)
                if live(1):
                    g, b = group(i, k, 1), (k - 1) % 2
                    now = mx[:, (k - 1) % 4, :]
                    dve.wait_ge(evac_done, g + 1)
                    if live(5):
                        dve.wait_ge(b_done, g - 3)
                    before = mx[:, (k - 2) % 4, GROUP - 1:GROUP] if live(2) else -BIG
                    nc.vector.tensor_tensor_scan(now, ps_cap[:, b, :], mt[:, b, :], before,
                                                 ALU.min, ALU.max).then_inc(scan_done, 1)
                if live(2):
                    window_match(oh[:, k % 2, :, :], i, k, 2, oh_done)
                if live(1):
                    dve.wait_ge(scan_done, g + 1)
                    back = mx[:, (k - 1) % 4, GROUP - 2::-1]
                    nc.vector.tensor_tensor_scan(back, ps_cap[:, b, GROUP - 1:0:-1], back,
                                                 mx[:, (k - 1) % 4, GROUP - 1:GROUP], ALU.min, ALU.max) \
                      .then_inc(rev_done, 1)
                if live(2):
                    b2 = k % 2
                    dve.wait_ge(exp_done, group(i, k, 2) + 1)
                    nc.vector.tensor_tensor(ec[:, b2, 1, :, :], m[:, (k - 2) % SLOTS, :, :],
                                            ec[:, b2, 0, :, :], ALU.mult).then_inc(mul_done, 1)
                if live(1):
                    c = (k - 1) % 4
                    dve.wait_ge(rev_done, g + 1)
                    if live(5):
                        dve.wait_ge(fac_done, g - 3)
                    first = mx[:, c, 0:1]
                    nc.vector.scalar_tensor_tensor(out=drop[:, c:c + 1], in0=first,
                                                   scalar=(mx[:, (k - 2) % 4, GROUP - 1:GROUP] if live(2)
                                                           else 0.0),
                                                   in1=first, op0=ALU.min, op1=ALU.subtract) \
                      .then_inc(drop_done, 1)
                if live(3):
                    g, b, c = group(i, k, 3), (k - 3) % 2, (k - 3) % 4
                    start = window_start(i, k, 3)
                    dve.wait_ge(fac_done, g + 1)
                    if live(4):
                        dve.wait_ge(added, g)
                    head = acc_t[:, :, bass.ds(start, 1)]
                    nc.vector.tensor_scalar(head, head, fac[:, c:c + 1], None, ALU.mult).then_inc(rescaled, 1)
                    dve.wait_ge(rescaled, g + 1)
                    dve.wait_ge(sums_done, g + 1)
                    cols = acc_t[:, :, bass.ds(start, WINDOW)]
                    nc.vector.tensor_tensor(cols, cols, ps_sum[:, b, 0:2 * WINDOW]
                                            .rearrange("p (q w) -> p q w", q=2), ALU.add).then_inc(added, 1)

            pipeline(dve, step, 3)

            dve.wait_ge(added, G)
            dve.wait_ge(r_done, 1)
            dve.wait_ge(w_loaded, 16 * 3)

            def aggregate(c, ch):
                n0, n1 = ch[0] * NP_, (ch[-1] + 1) * NP_
                dve.wait_ge(guess_done, c + 1)
                nc.vector.tensor_tensor(acc_t[:, 0, n0:n1], acc_t[:, 0, n0:n1], guess[:, n0:n1], ALU.mult) \
                  .then_inc(check_done, 1)
                dve.wait_ge(check_done, c + 1)
                dve.wait_ge(quot_done, c + 1)
                nc.vector.scalar_tensor_tensor(out=acc_t[:, 1, n0:n1], in0=acc_t[:, 0, n0:n1], scalar=2.0,
                                               in1=acc_t[:, 1, n0:n1], op0=ALU.subtract, op1=ALU.mult,
                                               reverse0=True).then_inc(agg_done, 1)

            def finish(c, ch):
                a0, a1 = ch[0], ch[-1] + 1
                dve.wait_ge(mlp_done, c + 1)
                t = tmp[:, c % 2, 0:a1 - a0, :]
                nc.vector.scalar_tensor_tensor(
                    out=t, in0=mlp_bank(c)[:, 0:(a1 - a0) * D].rearrange("p (a c) -> p a c", c=D),
                    scalar=0.0, in1=scale_bc[0:NP_, :].rearrange("p (a c) -> p a c", a=1)
                    .to_broadcast([NP_, a1 - a0, D]), op0=ALU.max, op1=ALU.mult).then_inc(relu_done, 1)
                dve.wait_ge(relu_done, c + 1)
                nc.vector.tensor_tensor(rs[:, a0:a1, :], t, rs[:, a0:a1, :], ALU.add).then_inc(out_done, 1)

            for c, ch in enumerate(CHUNKS):
                aggregate(c, ch)
                if c >= 1:
                    finish(c - 1, CHUNKS[c - 1])
            finish(NCH - 1, CHUNKS[-1])


_INS = ['x', 'src', 'dst', 'edge_attr_128', 'edge_weight', 'L1_gnn_mlp_w', 'L1_gnn_mlp_b', 'L1_gnn_scale']
_OUTS = [((3125, 128), 'float32')]


def kernel(**inputs):
    import numpy as _np
    import concourse.bacc as _bacc
    from concourse import mybir as _mybir
    from concourse.bass_utils import run_bass_kernel_spmd as _run

    nc = _bacc.Bacc("TRN2", target_bir_lowering=False, num_devices=1)
    arrays, args = {}, []
    for name in _INS:
        a = _np.ascontiguousarray(inputs[name])
        arrays[f"in_{name}_dram"] = a
        args.append(nc.dram_tensor(f"in_{name}_dram", a.shape, _mybir.dt.from_np(a.dtype),
                                   kind="ExternalInput").ap())
    for i, (shape, dtype) in enumerate(_OUTS):
        dt = _mybir.dt.from_np(_np.dtype(dtype))
        args.append(nc.dram_tensor(f"out_{i}_dram", shape, dt, kind="ExternalOutput").ap())
    gnn_kernel(nc, *args)
    r = _run(nc, [arrays], core_ids=[0])
    return r.results[0]["out_0_dram"]
```

```python
from contextlib import ExitStack

import concourse.bass as bass
from concourse import mybir

F32 = mybir.dt.float32
BF16 = mybir.dt.bfloat16
I32 = mybir.dt.int32
ALU = mybir.AluOpType
ACT = mybir.ActivationFunctionType

P = 128
LANES = 4
GROUP = P * LANES
SLOTS = 8
WINDOW = 64
AHEAD = 4
CHUNK = 4
SIDES = 3
EPS = 1e-5
BIG = 1.7e38
TINY = 1e-18


def gnn_kernel(nc, x, src, dst, edge_attr, edge_weight, mlp_w, mlp_b, scale, out):
    N, D = x.shape
    E = src.shape[0]
    NBLK = 25
    NP_ = N // NBLK
    assert NP_ * NBLK == N and NP_ <= P and D == P
    G = -(-E // GROUP)
    assert G % SLOTS == 0 and G <= P
    FULL = E // GROUP
    REST = E - FULL * GROUP
    RESTP, RESTJ = REST // LANES, REST % LANES
    assert FULL == G - 1 and REST > 0
    COLS = N + WINDOW
    CHUNKS = [list(range(a, min(a + CHUNK, NBLK))) for a in range(0, NBLK, CHUNK)]
    NCH = len(CHUNKS)
    OUTS = [list(range(a, min(a + 3, NBLK))) for a in range(0, NBLK, 3)]
    NOUT = len(OUTS)
    EARLY = 4
    EARLY_NODES = EARLY * 3 * NP_
    EARLY_GROUPS = G - 2 * SLOTS - 3

    h_table = nc.dram_tensor("h_table", [N + WINDOW, D], F32, kind="Internal").ap()
    side_tables = [nc.dram_tensor(f"side_table{j}", [N + P, D], F32, kind="Internal").ap()
                   for j in range(LANES)]
    h2_table = nc.dram_tensor("h2_table", [N, D], F32, kind="Internal").ap()

    def blocks(t):
        return t.rearrange("(a p) c -> p a c", p=NP_)

    with ExitStack() as ctx:
        def sb(name, shape, dt=F32):
            return ctx.enter_context(nc.sbuf_tensor(name, shape, dt))

        def psum(name, shape, dt=F32):
            return ctx.enter_context(nc.psum_tensor(name, shape, dt))

        def sem(name):
            return ctx.enter_context(nc.semaphore(name))

        ident = sb("ident", [P, P])
        identb = sb("identb", [P, P], BF16)
        iota_w = sb("iota_w", [P, WINDOW])
        below = sb("below", [P, P])
        spare = sb("spare", [P, 1])
        eps_col = sb("eps_col", [P, 1])
        tiny_col = sb("tiny_col", [P, 1])
        warm = sb("warm", [P, 1])
        src_g = sb("src_g", [G, GROUP], I32)
        dst_g = sb("dst_g", [G, GROUP], I32)
        prev_g = sb("prev_g", [G, GROUP], I32)
        w_g = sb("w_g", [G, GROUP])
        src_f = sb("src_f", [G, GROUP])
        dst_f = sb("dst_f", [G, GROUP])
        rel_f = sb("rel_f", [G, GROUP])
        same_f = sb("same_f", [G, GROUP])
        cap_g = sb("cap_g", [G, GROUP], BF16)
        lo_i = sb("lo_i", [G, GROUP], I32)
        hi_i = sb("hi_i", [G, GROUP], I32)
        lo_g = sb("lo_g", [G, GROUP], BF16)
        hi_g = sb("hi_g", [G, GROUP], BF16)
        idx_t = sb("idx_t", [P, G + SLOTS, LANES])
        rel_t = sb("rel_t", [P, G, LANES])
        w_t = sb("w_t", [P, G, LANES])
        to_spare = sb("to_spare", [P, G, LANES])
        base_row = sb("base_row", [1, G], I32)
        late_row = sb("late_row", [1, G], I32)
        idx0 = sb("idx0", [P, SLOTS, LANES], I32)
        idx1 = sb("idx1", [P, SLOTS, LANES], I32)
        xs = sb("xs", [NP_, NBLK, D])
        hs = sb("hs", [NP_, NBLK, D])
        rs = sb("rs", [NP_, NBLK, D])
        stats = sb("stats", [NP_, NBLK, 6])
        meanvar = sb("meanvar", [NP_, NBLK, 2])
        std = sb("std", [NP_, NBLK])
        rstd = sb("rstd", [NP_, NBLK])
        shift = sb("shift", [NP_, NBLK])
        acc_t = sb("acc_t", [P, 2, COLS])
        hwin = sb("hwin", [WINDOW, SLOTS, D])
        msg = sb("msg", [P, SLOTS, LANES, D])
        equal = sb("equal", [P, 2, LANES, P])
        earlier = sb("earlier", [P, LANES, P])
        count = sb("count", [P, 2, LANES])
        away = sb("away", [P, 2, LANES])
        oh0 = sb("oh0", [P, 2, LANES, WINDOW])
        ohw = sb("ohw", [P, 2, LANES, WINDOW])
        mix = sb("mix", [WINDOW, 2, LANES, P])
        side_in = sb("side_in", [P, SIDES, LANES - 1, CHUNK, D])
        pair = sb("pair", [NP_, 2, CHUNK, D])
        triple = sb("triple", [NP_, 2, CHUNK, D])
        m = sb("m", [P, SLOTS, LANES, D])
        mt = sb("mt", [P, 2, GROUP])
        mx = sb("mx", [P, 4, GROUP])
        ec = sb("ec", [P, 2, 2, LANES, D])
        oh = sb("oh", [P, 2, LANES, WINDOW])
        drop = sb("drop", [P, 4])
        fac = sb("fac", [P, 4])
        spent = side_in[:, :, :, :, :].rearrange("p s t a c -> p (s t a c)")
        guess = spent[:, 0:N]
        hidden = guess
        w_sb = sb("w_sb", [D, D])
        w_tr = sb("w_tr", [D, D])
        b_col = sb("b_col", [D, 1])
        scale_col = sb("scale_col", [D, 1])
        scale_diag = sb("scale_diag", [D, D])
        reach = sb("reach", [G, 1])
        furthest = sb("furthest", [1, 1])
        lack = sb("lack", [1, 1])
        beyond = sb("beyond", [1, 1], I32)
        ends = sb("ends", [1, 2, GROUP], I32)
        h_cols = m[:, :, :, :].rearrange("p s j c -> p (s j c)")[:, 0:N]
        top = msg[:, :, :, :].rearrange("p s j c -> p (s j c)")[:, 0:N]
        ea_rows = equal[:, 0, :, :]
        ea_cols = mt[:, 0, :]
        weights = mt[:, 1, :]
        terms = ec[:, 0, :, :, :].rearrange("p q j c -> p q (j c)")

        ps_mt = psum("ps_mt", [P, 2, GROUP])
        ps_cap = psum("ps_cap", [P, 2, GROUP])
        ps_b = psum("ps_b", [P, 2, LANES, D])
        ps_sum = psum("ps_sum", [P, 2, GROUP])

        chunk_loaded = [sem(f"chunk_loaded{c}") for c in range(NCH)]
        lists_set = sem("lists_set")
        lists_loaded = sem("lists_loaded")
        prev_loaded = sem("prev_loaded")
        side0_loaded = sem("side0_loaded")
        side0_done = sem("side0_done")
        w_loaded = sem("w_loaded")
        idents_zero = sem("idents_zero")
        idents_ready = sem("idents_ready")
        below_ones = sem("below_ones")
        window_cols = sem("window_cols")
        spares_ready = sem("spares_ready")
        eps_ready = sem("eps_ready")
        acc_zero = sem("acc_zero")
        stats_done = sem("stats_done")
        aggr_done = sem("aggr_done")
        std_done = sem("std_done")
        rstd_done = sem("rstd_done")
        shift_done = sem("shift_done")
        h_raw = sem("h_raw")
        h_last = sem("h_last")
        h_done = sem("h_done")
        xh_done = sem("xh_done")
        h_written = sem("h_written")
        src_real = sem("src_real")
        dst_real = sem("dst_real")
        rel_done = sem("rel_done")
        digits_split = sem("digits_split")
        digits_ready = sem("digits_ready")
        same_done = sem("same_done")
        caps_ready = sem("caps_ready")
        src_turned = sem("src_turned")
        rel_turned = sem("rel_turned")
        w_turned = sem("w_turned")
        base_turned = sem("base_turned")
        mlp_turned = sem("mlp_turned")
        idx_ready = sem("idx_ready")
        rel_ready = sem("rel_ready")
        weights_ready = sem("weights_ready")
        base_ready = sem("base_ready")
        spare_ready = sem("spare_ready")
        mlp_ready = sem("mlp_ready")
        scatter_open = sem("scatter_open")
        gather_open = sem("gather_open")
        zeroed = sem("zeroed")
        pad_cleared = sem("pad_cleared")
        side_cleared = [sem(f"side_cleared{j}") for j in range(LANES)]
        win_loaded = [sem(f"win_loaded{s}") for s in range(SLOTS)]
        src_spread = sem("src_spread")
        equal_done = sem("equal_done")
        oh0_done = sem("oh0_done")
        ohw_done = sem("ohw_done")
        count_done = sem("count_done")
        away_done = sem("away_done")
        idx0_ready = sem("idx0_ready")
        mix_summed = sem("mix_summed")
        mix_done = sem("mix_done")
        msg_summed = sem("msg_summed")
        msg_ready = sem("msg_ready")
        scattered = [sem(f"scattered{j}") for j in range(LANES)]
        pairs_done = sem("pairs_done")
        sides_done = sem("sides_done")
        x1_done = sem("x1_done")
        stats1_done = sem("stats1_done")
        aggr1_done = sem("aggr1_done")
        std1_done = sem("std1_done")
        rstd1_done = sem("rstd1_done")
        shift1_done = sem("shift1_done")
        h2_done = sem("h2_done")
        r_done = sem("r_done")
        h2_written = sem("h2_written")
        idx1_ready = sem("idx1_ready")
        ea_loaded = [sem(f"ea_loaded{s}") for s in range(SLOTS)]
        rest_loaded = sem("rest_loaded")
        m_ready = [sem(f"m_ready{s}") for s in range(SLOTS)]
        mt_done = sem("mt_done")
        caps_spread = sem("caps_spread")
        evac_done = sem("evac_done")
        scan_done = sem("scan_done")
        rev_done = sem("rev_done")
        drop_done = sem("drop_done")
        fac_done = sem("fac_done")
        b_done = sem("b_done")
        sub_done = sem("sub_done")
        exp_done = sem("exp_done")
        mul_done = sem("mul_done")
        oh_done = sem("oh_done")
        sums_done = sem("sums_done")
        rescaled = sem("rescaled")
        added = sem("added")
        ln_done = sem("ln_done")
        guess_done = sem("guess_done")
        quot_done = sem("quot_done")
        check_done = sem("check_done")
        agg_done = sem("agg_done")
        mlp_done = sem("mlp_done")
        relu_done = sem("relu_done")
        back_done = sem("back_done")
        out_done = sem("out_done")
        out_written = sem("out_written")
        reach_done = sem("reach_done")
        reach_turned = sem("reach_turned")
        beyond_ready = sem("beyond_ready")
        again_loaded = sem("again_loaded")
        cols_turned = sem("cols_turned")
        cols_taken = sem("cols_taken")
        side_summed = sem("side_summed")
        rows_turned = sem("rows_turned")
        rows_taken = sem("rows_taken")
        var_ready = sem("var_ready")
        root_ready = sem("root_ready")
        h2_again = sem("h2_again")
        staging_free = sem("staging_free")
        edges_loaded = sem("edges_loaded")
        ea_turned = sem("ea_turned")
        loop_open = sem("loop_open")
        z_ready = sem("z_ready")
        e_ready = sem("e_ready")
        agg_again = sem("agg_again")
        mlp_again = sem("mlp_again")
        relu_again = sem("relu_again")
        back_again = sem("back_again")
        out_again = sem("out_again")
        out_rewritten = sem("out_rewritten")

        block = ctx.enter_context(nc.Block())

        def pipeline(eng, step, lag, peel=1, early=None):
            for n in range(SLOTS * peel):
                step(n // SLOTS, n % SLOTS, lambda d, n=n: n - d >= 0)
            with eng.Fori(peel, G // SLOTS - (2 if early else 0)) as i:
                for k in range(SLOTS):
                    step(i, k, lambda d: d <= SLOTS * peel)
            if early:
                for t in range(2 * SLOTS):
                    step(G // SLOTS - 2 + t // SLOTS, t % SLOTS, lambda d: d <= SLOTS * peel)
                    early(t)
            for k in range(lag):
                step(G // SLOTS, k, lambda d, k=k: d > k)
                if early:
                    early(2 * SLOTS + k)

        CLOSING = 5

        def table_of(g, j):
            if g == 0:
                return (2, 0, 1, 2)[j]
            return 1 + (LANES * g + j) % 3 if g >= G - CLOSING else j

        assert LANES == 4 and (G - CLOSING) * LANES % 3 == 0

        def landed_after(t, g):
            if isinstance(g, int):
                return sum(table_of(a, j) == t for a in range(g) for j in range(LANES))
            return g + (sum(table_of(0, j) == t for j in range(LANES)) - 1)

        def mlp_bank(c, n):
            return ps_cap[:, 1, 0:n] if c < EARLY else ps_mt[:, c % 2, 0:n]

        def back_bank(c, n):
            return (ps_cap[0:NP_, c % 2, 0:n] if c % 4 < 2
                    else ps_b[0:NP_, c % 2, :, :].rearrange("p j e -> p (j e)")[:, 0:n])

        def guesses(c):
            return 1 if c < EARLY else c - EARLY + 2

        def use(i, k, d=0):
            return i if k >= d else i - 1

        def group(i, k, d=0):
            return i * SLOTS + (k - d)

        LOADS = (3, 2 + LANES, 2 + LANES)

        def free_count(t, g):
            return g + (1 + t * (G + 1))

        def loads_count(t, g):
            return 16 * LOADS[t] * (g + 1) + 16 * G * sum(LOADS[:t])

        def out_of_windows(eng):
            eng.wait_ge(beyond_ready, 1)
            return eng.value_load(beyond[0:1, 0:1], min_val=0, max_val=1) > 0

        def each_group(eng, body):
            with eng.Fori(0, FULL) as g:
                body(g, GROUP)
            body(FULL, REST)

        def lanes_of(n):
            return [(j, min(P, n - j * P)) for j in range(LANES)]

        assert REST > (LANES - 1) * P

        @block.sync
        def _(sp):
            def load_x(c):
                a0, a1 = CHUNKS[c][0], CHUNKS[c][-1] + 1
                sp.dma_start(xs[:, a0:a1, :], blocks(x)[:, a0:a1, :]).then_inc(chunk_loaded[c], 16)

            for c in range(NCH):
                load_x(c)
            sp.wait_ge(lists_set, 4)
            for t, v in ((dst_g, dst), (src_g, src), (w_g, edge_weight)):
                sp.dma_start(t[0:FULL, :], v[0:FULL * GROUP].rearrange("(g e) -> g e", e=GROUP)) \
                  .then_inc(lists_loaded, 16)
                sp.dma_start(t[FULL:G, 0:REST], v[FULL * GROUP:E].rearrange("(g e) -> g e", g=1)) \
                  .then_inc(lists_loaded, 16)
            sp.wait_ge(zeroed, 1)
            sp.dma_start(h_table[N:N + WINDOW, :], rs[0:WINDOW, 0, :]).then_inc(pad_cleared, 16)

            def clear_side(j):
                t = side_tables[j]
                sp.dma_start(blocks(t[0:N, :]), rs[:, :, :]).then_inc(side_cleared[j], 16)
                sp.dma_start(t[N:N + P, :].rearrange("(p a) c -> p a c", a=2), rs[0:P // 2, 0:2, :]) \
                  .then_inc(side_cleared[j], 16)

            clear_side(2)
            clear_side(0)
            for c, ch in enumerate(CHUNKS):
                sp.wait_ge(h_done, ch[-1] - c)
                sp.wait_ge(h_last, c + 1)
                sp.dma_start(blocks(h_table[0:N, :])[:, ch[0]:ch[-1] + 1, :],
                             hs[:, ch[0]:ch[-1] + 1, :]).then_inc(h_written, 16)

            def load_group(slot, rows):
                sp.dma_start(m[:, slot, :, :], rows.rearrange("(p j) c -> p j c", j=LANES)) \
                  .then_inc(ea_loaded[slot], 16)

            sp.wait_ge(base_ready, 1)

            def load_window(i, k, live):
                g = group(i, k)
                if live(SLOTS):
                    sp.wait_ge(msg_summed, g - SLOTS + 1)
                start = sp.value_load(base_row[0:1, bass.ds(g, 1)], min_val=0, max_val=N - 1)
                if not live(1):
                    sp.wait_ge(h_written, 16 * NCH)
                    sp.wait_ge(pad_cleared, 16)
                sp.dma_start(hwin[:, k, :], h_table[bass.ds(start, WINDOW), :]).then_inc(win_loaded[k], 16)
                if live(SLOTS):
                    return
                if k == 0:
                    clear_side(1)
                if k == 3:
                    clear_side(3)
                if k == SLOTS - 1:
                    sp.dma_start(prev_g[0:1, 1:GROUP], dst[0:GROUP - 1].rearrange("(g e) -> g e", g=1)) \
                      .then_inc(prev_loaded, 16)
                    sp.dma_start(prev_g[1:FULL, :],
                                 dst[GROUP - 1:FULL * GROUP - 1].rearrange("(g e) -> g e", e=GROUP)) \
                      .then_inc(prev_loaded, 16)
                    sp.dma_start(prev_g[FULL:G, 0:REST + 1],
                                 dst[FULL * GROUP - 1:E].rearrange("(g e) -> g e", g=1)) \
                      .then_inc(prev_loaded, 16)

            pipeline(sp, load_window, 0)
            for s in range(SLOTS):
                load_group(s, edge_attr[s * GROUP:(s + 1) * GROUP, :])

            for j in range(LANES):
                sp.wait_ge(side_cleared[j], 32)
            sp.wait_ge(scattered[0], 16 * landed_after(0, G))
            for a in range(NBLK):
                sp.dma_start(rs[:, a, :], side_tables[0][a * NP_:(a + 1) * NP_, :]).then_inc(side0_loaded, 16)
            for t in range(1, LANES):
                sp.wait_ge(scattered[t], 16 * landed_after(t, G))
            for c, ch in enumerate(CHUNKS):
                if c >= SIDES:
                    sp.wait_ge(sides_done, c - SIDES + 1)
                for j, t in enumerate(side_tables[1:]):
                    sp.dma_start(side_in[0:NP_, c % SIDES, j, 0:len(ch), :],
                                 blocks(t[0:N, :])[:, ch[0]:ch[-1] + 1, :]).then_inc(chunk_loaded[c], 16)
            for c, ch in enumerate(CHUNKS):
                sp.wait_ge(h2_done, ch[-1] + 1)
                sp.dma_start(blocks(h2_table)[:, ch[0]:ch[-1] + 1, :],
                             hs[:, ch[0]:ch[-1] + 1, :]).then_inc(h2_written, 16)
            with sp.Fori(1, G // SLOTS - 1) as i:
                for k in range(SLOTS):
                    sp.wait_ge(mul_done, (i - 1) * SLOTS + k + 1)
                    load_group(k, edge_attr[bass.ds((i * SLOTS + k) * GROUP, GROUP), :])
            for k in range(SLOTS):
                g = G - SLOTS + k
                sp.wait_ge(mul_done, g - SLOTS + 1)
                if g < FULL:
                    load_group(k, edge_attr[g * GROUP:(g + 1) * GROUP, :])
                else:
                    rows = edge_attr[g * GROUP:g * GROUP + RESTP * LANES, :]
                    sp.dma_start(m[0:RESTP, k, :, :], rows.rearrange("(p j) c -> p j c", j=LANES)) \
                      .then_inc(ea_loaded[k], 16)
                    sp.dma_start(m[RESTP:RESTP + 1, k, 0:RESTJ, :],
                                 edge_attr[E - RESTJ:E, :].rearrange("(p j) c -> p j c", j=RESTJ)) \
                      .then_inc(rest_loaded, 16)
            for c, ch in enumerate(OUTS):
                sp.wait_ge(out_done, c + 1)
                sp.dma_start(blocks(out)[:, ch[0]:ch[-1] + 1, :],
                             rs[:, ch[0]:ch[-1] + 1, :]).then_inc(out_written, 16)
            sp.wait_ge(out_written, 16 * NOUT)

            with sp.If(out_of_windows(sp)):
                sp.dma_start(hs[:, :, :], blocks(h_table[0:N, :])).then_inc(again_loaded, 16)
                sp.dma_start(xs[:, :, :], blocks(x)).then_inc(again_loaded, 16)
                for t in range(3):
                    def load_edges(g, n):
                        sp.wait_ge(staging_free, free_count(t, g))
                        for q, v in enumerate((src, dst)):
                            sp.dma_start(ends[:, q, 0:n], v[bass.ds(g * GROUP, n)].rearrange("(a e) -> a e", a=1)) \
                              .then_inc(edges_loaded, 16)
                        if t == 0:
                            sp.dma_start(weights[:, 0:n], edge_weight[bass.ds(g * GROUP, n)]
                                         .rearrange("(a e) -> a e", a=1).to_broadcast([P, n])) \
                              .then_inc(edges_loaded, 16)
                            return
                        for j, r in lanes_of(n):
                            sp.dma_start(ea_rows[0:r, j, :], edge_attr[bass.ds(g * GROUP + j * P, r), :]) \
                              .then_inc(edges_loaded, 16)
                    each_group(sp, load_edges)
                sp.wait_ge(out_again, NOUT)
                sp.dma_start(blocks(out), rs[:, :, :]).then_inc(out_rewritten, 16)
                sp.wait_ge(out_rewritten, 16)

        @block.gpsimd
        def _(pool):
            nc.gpsimd.memset(dst_g[:, :], -1).then_inc(lists_set, 1)
            nc.gpsimd.memset(prev_g[:, :], -1).then_inc(lists_set, 1)
            nc.gpsimd.memset(src_g[:, :], 0).then_inc(lists_set, 1)
            nc.gpsimd.memset(w_g[:, :], 0.0).then_inc(lists_set, 1)
            nc.gpsimd.memset(rs[:, :, :], 0.0).then_inc(zeroed, 1)
            nc.gpsimd.memset(ident[:, :], 0.0).then_inc(idents_zero, 1)
            nc.gpsimd.memset(identb[:, :], 0.0).then_inc(idents_zero, 1)
            nc.gpsimd.memset(below[:, :], 1.0).then_inc(below_ones, 1)
            pool.wait_ge(idents_zero, 2)
            for t in (ident, identb):
                nc.gpsimd.affine_select(out=t[:, :], in_=t[:, :], compare_op=ALU.not_equal, fill=1.0, base=0,
                                        pattern=[[-1, P]], channel_multiplier=1).then_inc(idents_ready, 1)
            pool.wait_ge(below_ones, 1)
            nc.gpsimd.affine_select(out=below[:, :], in_=below[:, :], compare_op=ALU.is_gt, fill=0.0, base=0,
                                    pattern=[[-1, P]], channel_multiplier=1).then_inc(window_cols, 1)
            nc.gpsimd.iota(iota_w[:, :], pattern=[[1, WINDOW]], base=0, channel_multiplier=0,
                           allow_small_or_imprecise_dtypes=True).then_inc(window_cols, 1)
            nc.gpsimd.iota(spare[:, :], pattern=[[1, 1]], base=N, channel_multiplier=1,
                           allow_small_or_imprecise_dtypes=True).then_inc(window_cols, 1)
            nc.gpsimd.memset(idx_t[:, G:G + SLOTS, :], 0.0).then_inc(spares_ready, 1)

            def norm_last(c, ch, shift_sem, raw_sem, last_sem):
                a = ch[-1]
                pool.wait_ge(shift_sem, c + 1)
                nc.gpsimd.tensor_scalar(hs[:, a, :], xs[:, a, :], rstd[:, a:a + 1], shift[:, a:a + 1],
                                        ALU.mult, ALU.add).then_inc(raw_sem, 1)
                pool.wait_ge(raw_sem, c + 1)
                nc.gpsimd.tensor_scalar(hs[:, a, :], hs[:, a, :], 0.0, None, ALU.max).then_inc(last_sem, 1)

            for c, ch in enumerate(CHUNKS):
                norm_last(c, ch, shift_done, h_raw, h_last)

            def scatter0(g, k, table):
                pool.wait_ge(msg_ready, g + 1)
                pool.wait_ge(idx0_ready, g + 1)
                for j in range(LANES):
                    t = table(j)
                    if isinstance(g, int):
                        landed = landed_after(t, g) + sum(table(b) == t for b in range(j))
                    else:
                        landed = landed_after(t, g)
                    if isinstance(g, int) and landed == 0:
                        pool.wait_ge(side_cleared[t], 32)
                    else:
                        pool.wait_ge(scattered[t], landed * 16)
                    pool.sem_inc(scatter_open, 1)
                    nc.gpsimd.indirect_dma_start(
                        side_tables[t][:, :], bass.IndirectOffsetOnAxis(ap=idx0[:, k, j:j + 1], axis=0),
                        msg[:, k, j, :], None, compute_op=ALU.add).then_inc(scattered[t], 16)

            for g in range(SLOTS):
                scatter0(g, g, lambda j: table_of(g, j))
            with pool.Fori(1, G // SLOTS - 1) as i:
                for k in range(SLOTS):
                    scatter0(group(i, k), k, lambda j: j)
            for g in range(G - SLOTS, G):
                scatter0(g, g % SLOTS, lambda j: table_of(g, j))

            for c, ch in enumerate(CHUNKS):
                n = len(ch)
                pool.wait_ge(chunk_loaded[c], 16 * LANES)
                nc.gpsimd.tensor_tensor(pair[:, c % 2, 0:n, :], side_in[0:NP_, c % SIDES, 0, 0:n, :],
                                        side_in[0:NP_, c % SIDES, 1, 0:n, :], ALU.add).then_inc(pairs_done, 1)
                pool.wait_ge(pairs_done, c + 1)
                if c >= 2:
                    pool.wait_ge(x1_done, c - 1)
                nc.gpsimd.tensor_tensor(triple[:, c % 2, 0:n, :], pair[:, c % 2, 0:n, :],
                                        side_in[0:NP_, c % SIDES, 2, 0:n, :], ALU.add).then_inc(sides_done, 1)
            pool.wait_ge(h2_written, 16 * NCH)

            def gather1(i, k, live):
                pool.wait_ge(idx1_ready, group(i, k) + 1)
                pool.wait_ge(ea_loaded[k], (i + 1) * 16)
                pool.sem_inc(gather_open, 1)
                for j in range(LANES):
                    nc.gpsimd.indirect_dma_start(
                        m[:, k, j, :], None, h2_table[:, :],
                        bass.IndirectOffsetOnAxis(ap=idx1[:, k, j:j + 1], axis=0),
                        compute_op=ALU.add).then_inc(m_ready[k], 16)

            pipeline_last = G // SLOTS - 1
            for k in range(SLOTS):
                gather1(0, k, None)
            with pool.Fori(1, pipeline_last) as i:
                for k in range(SLOTS):
                    gather1(i, k, None)
            for k in range(SLOTS):
                if k == SLOTS - 1:
                    pool.wait_ge(rest_loaded, 16)
                gather1(pipeline_last, k, None)

            for c, ch in list(enumerate(OUTS))[EARLY:]:
                cols = acc_t[:, 1, ch[0] * NP_:(ch[-1] + 1) * NP_]
                pool.wait_ge(guess_done, guesses(c))
                nc.gpsimd.tensor_tensor(cols, cols, guess[:, ch[0] * NP_:(ch[-1] + 1) * NP_], ALU.mult) \
                  .then_inc(quot_done, 1)

        @block.scalar
        def _(act):
            def normalize(stat_sem, std_sem, shift_sem, done, left):
                def deviation(c):
                    a0, a1 = CHUNKS[c][0], CHUNKS[c][-1] + 1
                    act.wait_ge(stat_sem, a1)
                    nc.scalar.activation(std[:, a0:a1], meanvar[:, a0:a1, 1], ACT.Sqrt,
                                         bias=eps_col[0:NP_, 0:1]).then_inc(std_sem, 1)

                deviation(0)
                for c, ch in enumerate(CHUNKS):
                    if c + 1 < NCH:
                        deviation(c + 1)
                    act.wait_ge(shift_sem, c + 1)
                    for a in ch[:len(ch) - left]:
                        nc.scalar.activation(hs[:, a, :], xs[:, a, :], ACT.Relu, bias=shift[:, a:a + 1],
                                             scale=rstd[:, a:a + 1]).then_inc(done, 1)

            act.wait_ge(eps_ready, 2)
            nc.scalar.activation(warm[:, :], eps_col[:, :], ACT.Sqrt)
            normalize(aggr_done, std_done, shift_done, h_done, 1)

            act.dma_start(w_sb[:, :], mlp_w).then_inc(w_loaded, 16)
            act.dma_start(b_col[:, :], mlp_b.rearrange("(n a) -> n a", a=1)).then_inc(w_loaded, 16)
            act.dma_start(scale_col[:, :], scale.rearrange("(n a) -> n a", a=1)).then_inc(w_loaded, 16)

            def mix_and_messages(i, k, live):
                if live(2):
                    g, b = group(i, k, 2), k % 2
                    act.wait_ge(msg_summed, g + 1)
                    if live(2 + SLOTS):
                        act.wait_ge(scatter_open, (g - SLOTS + 2) * LANES)
                    nc.scalar.copy(msg[:, (k - 2) % SLOTS, :, :], ps_b[:, b, :, :]).then_inc(msg_ready, 1)
                if live(1):
                    g, b = group(i, k, 1), (k - 1) % 2
                    pe_done = mix_summed
                    act.wait_ge(pe_done, g + 1)
                    if live(3):
                        act.wait_ge(msg_summed, g - 1)
                    nc.scalar.copy(mix[:, b, :, :], ps_mt[0:WINDOW, b, :].rearrange("d (j e) -> d j e", j=LANES)) \
                      .then_inc(mix_done, 1)

            pipeline(act, mix_and_messages, 2, peel=2)

            act.wait_ge(idx_ready, 1)
            act.wait_ge(spares_ready, 1)
            for s in range(AHEAD):
                nc.scalar.copy(idx1[:, s, :], idx_t[:, s, :]).then_inc(idx1_ready, 1)
            act.wait_ge(h_written, 16 * NCH)
            nc.scalar.activation(warm[:, :], eps_col[:, :], ACT.Sqrt)
            normalize(aggr1_done, std1_done, shift1_done, h2_done, 0)
            nc.scalar.activation(warm[:, :], eps_col[:, :], ACT.Exp)

            def stage(i, k, live):
                s = (k + AHEAD) % SLOTS
                if live(SLOTS - AHEAD):
                    act.wait_ge(m_ready[s], (use(i, k, SLOTS - AHEAD) + 1) * 16 * LANES)
                nc.scalar.copy(idx1[:, s, :], idx_t[:, bass.ds(group(i, k) + AHEAD, 1), :]
                               .rearrange("p a j -> p (a j)")).then_inc(idx1_ready, 1)

            def step(i, k, live):
                if live(2):
                    g = group(i, k, 2)
                    act.wait_ge(sub_done, g + 1)
                    e = ec[:, k % 2, 0, :, :]
                    nc.scalar.activation(e, e, ACT.Exp).then_inc(exp_done, 1)
                if live(0):
                    g = group(i, k)
                    act.wait_ge(mt_done, g + 1)
                    if live(2):
                        act.wait_ge(scan_done, g - 1)
                    nc.scalar.copy(mt[:, k % 2, :], ps_mt[:, k % 2, :]).then_inc(evac_done, 1)
                    stage(i, k, live)
                if live(1):
                    g, c = group(i, k, 1), (k - 1) % 4
                    act.wait_ge(drop_done, g + 1)
                    if live(5):
                        act.wait_ge(added, g - 3)
                    nc.scalar.activation(fac[:, c:c + 1], drop[:, c:c + 1], ACT.Exp).then_inc(fac_done, 1)

            def relu(c, ch, mlp_sem, done):
                act.wait_ge(mlp_sem, c + 1)
                n0, n1 = ch[0] * NP_, (ch[-1] + 1) * NP_
                nc.scalar.activation(hidden[:, n0:n1], mlp_bank(c, n1 - n0), ACT.Relu, bias=b_col[:, 0:1]) \
                  .then_inc(done, 1)

            def ln(n0, n1):
                nc.scalar.activation(guess[:, n0:n1], acc_t[:, 0, n0:n1], ACT.Ln, bias=tiny_col[:, 0:1]) \
                  .then_inc(ln_done, 1)

            def exp_minus(n0, n1):
                nc.scalar.activation(guess[:, n0:n1], guess[:, n0:n1], ACT.Exp, scale=-1.0) \
                  .then_inc(guess_done, 1)

            def early(t):
                if t == 0:
                    act.wait_ge(added, EARLY_GROUPS)
                    ln(0, EARLY_NODES)
                if t == 2:
                    act.wait_ge(ln_done, 1)
                    exp_minus(0, EARLY_NODES)
                if (t - 5) // 2 in range(EARLY) and t % 2 == 1:
                    relu((t - 5) // 2, OUTS[(t - 5) // 2], mlp_done, relu_done)

            act.wait_ge(w_loaded, 16 * 3)
            pipeline(act, step, 2, early=early)

            act.wait_ge(added, G)
            for c in range(EARLY, NOUT):
                ln(OUTS[c][0] * NP_, (OUTS[c][-1] + 1) * NP_)
            for c in range(EARLY, NOUT):
                act.wait_ge(ln_done, guesses(c))
                exp_minus(OUTS[c][0] * NP_, (OUTS[c][-1] + 1) * NP_)
            for c in range(EARLY, NOUT):
                relu(c, OUTS[c], mlp_done, relu_done)

            with act.If(out_of_windows(act)):
                act.wait_ge(var_ready, 1)
                nc.scalar.activation(std[:, :], meanvar[:, :, 1], ACT.Sqrt, bias=eps_col[0:NP_, 0:1]) \
                  .then_inc(root_ready, 1)

                def exp_group(g, n):
                    act.wait_ge(z_ready, g + 1)
                    nc.scalar.activation(terms[:, 0, 0:n], terms[:, 1, 0:n], ACT.Exp).then_inc(e_ready, 1)

                each_group(act, exp_group)
                for c, ch in enumerate(OUTS):
                    relu(c, ch, mlp_again, relu_again)

        @block.tensor
        def _(pe):
            pe.wait_ge(idents_ready, 2)
            for t, bank, loaded, count_, done in (
                    (src_f, ps_mt[:, 0, :], src_real, 1, src_turned), (rel_f, ps_mt[:, 1, :], rel_done, 1, rel_turned),
                    (w_g, ps_cap[:, 0, :], lists_loaded, 16 * 6, w_turned)):
                pe.wait_ge(loaded, count_)
                for j in range(LANES):
                    mm = pe.transpose(bank[:, j * G:(j + 1) * G], t[:, j::LANES], ident[0:G, 0:G])
                mm.then_inc(done, 1)
            pe.transpose(ps_cap[0:1, 1, 0:G], dst_f[:, 0:1], ident[0:G, 0:G]).then_inc(base_turned, 1)

            pe.wait_ge(digits_ready, 2)
            pe.wait_ge(idx_ready, 1)
            pe.wait_ge(rel_ready, 1)
            pe.wait_ge(weights_ready, 1)
            pe.wait_ge(base_ready, 1)

            def messages(i, k, live):
                if live(2):
                    g, b = group(i, k, 2), k % 2
                    pe.wait_ge(mix_done, g + 1)
                    pe.wait_ge(win_loaded[(k - 2) % SLOTS], (use(i, k, 2) + 1) * 16)
                    if live(4):
                        pe.wait_ge(msg_ready, g - 1)
                    for j in range(LANES):
                        mm = pe.matmul(ps_b[:, b, j, :], mix[:, b, j, :], hwin[:, (k - 2) % SLOTS, :],
                                       start=True, stop=True)
                    mm.then_inc(msg_summed, 1)
                if live(0):
                    g, b = group(i, k), k % 2
                    if live(2):
                        pe.wait_ge(equal_done, g - 1)
                    pick = identb[0:G, bass.ds(g, 1)].to_broadcast([G, P])
                    pe.matmul(ps_cap[:, b, :], pick, hi_g[:, :], start=True, stop=False)
                    pe.matmul(ps_cap[:, b, :], pick, lo_g[:, :], start=False, stop=True) \
                      .then_inc(src_spread, 1)
                if live(1):
                    g, b = group(i, k, 1), (k - 1) % 2
                    pe.wait_ge(equal_done, g + 1)
                    pe.wait_ge(ohw_done, g + 1)
                    if live(3):
                        pe.wait_ge(mix_done, g - 1)
                    for j in range(LANES):
                        mm = pe.matmul(ps_mt[0:WINDOW, b, j * P:(j + 1) * P], ohw[:, b, j, :],
                                       equal[:, b, j, :], start=True, stop=True)
                    mm.then_inc(mix_summed, 1)

            pipeline(pe, messages, 2)
            pe.wait_ge(msg_ready, G)
            pe.wait_ge(w_loaded, 16 * 3)
            pe.transpose(ps_sum[:, 0, 0:D], w_sb[:, :], ident[:, :]).then_inc(mlp_turned, 1)
            pe.wait_ge(reach_done, 4)
            pe.transpose(ps_sum[0:1, 1, 0:G], reach[:, :], ident[0:G, 0:G]).then_inc(reach_turned, 1)
            pe.wait_ge(caps_ready, 1)
            pe.wait_ge(mlp_ready, 2)
            pe.wait_ge(beyond_ready, 1)

            def step(i, k, live):
                if live(0):
                    g, b = group(i, k), k % 2
                    pe.wait_ge(m_ready[k], (i + 1) * 16 * LANES)
                    if live(2):
                        pe.wait_ge(evac_done, g - 1)
                    for j in range(LANES):
                        mm = pe.transpose(ps_mt[:, b, j::LANES], m[:, k, j, :], ident[:, :])
                    mm.then_inc(mt_done, 1)
                if live(1):
                    pe.wait_ge(rev_done, group(i, k, 1) + 1)
                if live(0):
                    pick = identb[0:G, bass.ds(group(i, k), 1)].to_broadcast([G, P])
                    pe.matmul(ps_cap[:, 0, :], pick, cap_g[:, :], start=True, stop=True) \
                      .then_inc(caps_spread, 1)
                if live(1):
                    g, b = group(i, k, 1), (k - 1) % 2
                    if live(3):
                        pe.wait_ge(sub_done, g - 1)
                    for j in range(LANES):
                        mm = pe.transpose(ps_b[:, b, j, :], mx[:, (k - 1) % 4, j::LANES], ident[:, :])
                    mm.then_inc(b_done, 1)
                if live(2):
                    g, b = group(i, k, 2), k % 2
                    pe.wait_ge(mul_done, g + 1)
                    pe.wait_ge(oh_done, g + 1)
                    if live(4):
                        pe.wait_ge(added, g - 1)
                    for q in range(2):
                        for j in range(LANES):
                            mm = pe.matmul(ps_sum[:, b, q * WINDOW:(q + 1) * WINDOW], ec[:, b, q, j, :],
                                           oh[:, b, j, :], start=(j == 0), stop=(j == LANES - 1))
                    mm.then_inc(sums_done, 1)

            def mlp(c, ch, relu_sem, done):
                n0, n1 = ch[0] * NP_, (ch[-1] + 1) * NP_
                before = c if c < EARLY else c - 1
                if before > 0 and c not in (EARLY, EARLY + 1):
                    pe.wait_ge(relu_sem, before)
                pe.matmul(mlp_bank(c, n1 - n0), w_tr[:, :], acc_t[:, 1, n0:n1], start=True, stop=True) \
                  .then_inc(done, 1)

            def scale_back(c, ch, relu_sem, out_sem, done):
                pe.wait_ge(relu_sem, c + 1)
                if c >= 4:
                    pe.wait_ge(out_sem, c - 3)
                bank = back_bank(c, len(ch) * D)
                for q in range(len(ch)):
                    mm = pe.matmul(bank[:, q * D:(q + 1) * D], hidden[:, ch[q] * NP_:(ch[q] + 1) * NP_],
                                   scale_diag[:, :], start=True, stop=True)
                mm.then_inc(done, 1)

            def early(t):
                if (t - 4) // 2 in range(EARLY) and t % 2 == 0:
                    c = (t - 4) // 2
                    pe.wait_ge(agg_done, c + 1)
                    mlp(c, OUTS[c], relu_done, mlp_done)

            pipeline(pe, step, 2, early=early)

            pe.wait_ge(relu_done, EARLY)
            for c in range(EARLY):
                scale_back(c, OUTS[c], relu_done, out_done, back_done)
            for c in range(EARLY, NOUT):
                pe.wait_ge(agg_done, c + 1)
                mlp(c, OUTS[c], relu_done, mlp_done)
                if c > EARLY:
                    scale_back(c - 1, OUTS[c - 1], relu_done, out_done, back_done)
            scale_back(NOUT - 1, OUTS[-1], relu_done, out_done, back_done)

            with pe.If(out_of_windows(pe)):
                def turn_nodes(before):
                    for c, ch in enumerate(CHUNKS):
                        if c >= 2:
                            pe.wait_ge(cols_taken, before + c - 1)
                        for q, a in enumerate(ch):
                            mm = pe.transpose(ps_mt[:, c % 2, q * NP_:(q + 1) * NP_], hs[:, a, :],
                                              ident[0:NP_, 0:NP_])
                        mm.then_inc(cols_turned, 1)

                pe.wait_ge(again_loaded, 32)
                turn_nodes(0)
                pe.wait_ge(side_summed, 1)
                for c, ch in enumerate(CHUNKS):
                    if c >= 2:
                        pe.wait_ge(rows_taken, c - 1)
                    for q, a in enumerate(ch):
                        mm = pe.transpose(ps_cap[0:NP_, c % 2, q * D:(q + 1) * D],
                                          acc_t[:, 0, a * NP_:(a + 1) * NP_], ident[:, :])
                    mm.then_inc(rows_turned, 1)
                pe.wait_ge(h2_again, 1)
                turn_nodes(NCH)
                for t in (1, 2):
                    def turn_edges(g, n):
                        pe.wait_ge(edges_loaded, loads_count(t, g))
                        for j, r in lanes_of(n):
                            mm = pe.transpose(ps_b[:, 0, j, 0:r], ea_rows[0:r, j, :], ident[0:r, 0:r])
                        mm.then_inc(ea_turned, 1)

                    each_group(pe, turn_edges)
                pe.wait_ge(agg_again, 1)
                for c, ch in enumerate(OUTS):
                    if c >= 1:
                        pe.wait_ge(out_again, c)
                    mlp(c, ch, relu_again, mlp_again)
                    scale_back(c, ch, relu_again, out_again, back_again)

        @block.vector
        def _(dve):
            nc.vector.memset(eps_col[:, :], EPS).then_inc(eps_ready, 1)
            nc.vector.memset(tiny_col[:, :], TINY).then_inc(eps_ready, 1)

            def norm_stats(c, ch, stats_sem, aggr_sem):
                for a in ch:
                    nc.vector.bn_stats(stats[:, a, :], xs[:, a, :]).then_inc(stats_sem, 1)
                dve.wait_ge(stats_sem, ch[-1] + 1)
                for a in ch:
                    nc.vector.bn_aggr(meanvar[:, a, :], stats[:, a, :]).then_inc(aggr_sem, 1)

            def norm_scale(c, ch, std_sem, rstd_sem, shift_sem):
                a0, a1 = ch[0], ch[-1] + 1
                dve.wait_ge(std_sem, c + 1)
                nc.vector.reciprocal(rstd[:, a0:a1], std[:, a0:a1]).then_inc(rstd_sem, 1)
                dve.wait_ge(rstd_sem, c + 1)
                nc.vector.scalar_tensor_tensor(out=shift[:, a0:a1], in0=meanvar[:, a0:a1, 0], scalar=-1.0,
                                               in1=rstd[:, a0:a1], op0=ALU.mult, op1=ALU.mult) \
                  .then_inc(shift_sem, 1)

            def lists_to_float():
                dve.wait_ge(lists_loaded, 16 * 6)
                nc.vector.tensor_copy(dst_f[:, :], dst_g[:, :]).then_inc(dst_real, 1)
                nc.vector.tensor_copy(src_f[:, :], src_g[:, :]).then_inc(src_real, 1)
                dve.wait_ge(dst_real, 1)
                nc.vector.tensor_scalar(rel_f[:, :], dst_f[:, :], dst_f[:, 0:1], None, ALU.subtract) \
                  .then_inc(rel_done, 1)
                nc.vector.tensor_scalar(lo_i[:, :], src_g[:, :], WINDOW - 1, None, ALU.bitwise_and) \
                  .then_inc(digits_split, 1)
                nc.vector.tensor_scalar(hi_i[:, :], src_g[:, :], -WINDOW, None, ALU.bitwise_and) \
                  .then_inc(digits_split, 1)
                dve.wait_ge(digits_split, 1)
                nc.vector.tensor_copy(lo_g[:, :], lo_i[:, :]).then_inc(digits_ready, 1)
                dve.wait_ge(digits_split, 2)
                nc.vector.tensor_copy(hi_g[:, :], hi_i[:, :]).then_inc(digits_ready, 1)

            for c, ch in enumerate(CHUNKS):
                dve.wait_ge(chunk_loaded[c], 16)
                norm_stats(c, ch, stats_done, aggr_done)
                if c >= 1:
                    norm_scale(c - 1, CHUNKS[c - 1], std_done, rstd_done, shift_done)
                if c == NCH - 2:
                    lists_to_float()
            norm_scale(NCH - 1, CHUNKS[-1], std_done, rstd_done, shift_done)

            def turned(bank):
                return bank[:, 0:LANES * G].rearrange("p (j g) -> p g j", j=LANES)

            dve.wait_ge(src_turned, 1)
            nc.vector.tensor_copy(idx_t[:, 0:G, :], turned(ps_mt[:, 0, :])).then_inc(idx_ready, 1)
            dve.wait_ge(rel_turned, 1)
            nc.vector.tensor_copy(rel_t[:, :, :], turned(ps_mt[:, 1, :])).then_inc(rel_ready, 1)
            dve.wait_ge(w_turned, 1)
            nc.vector.tensor_copy(w_t[:, :, :], turned(ps_cap[:, 0, :])).then_inc(weights_ready, 1)
            dve.wait_ge(base_turned, 1)
            nc.vector.tensor_copy(base_row[:, :], ps_cap[0:1, 1, 0:G]).then_inc(base_ready, 1)
            dve.wait_ge(window_cols, 3)
            dve.wait_ge(idx_ready, 1)
            nc.vector.tensor_scalar(to_spare[:, :, :], idx_t[:, 0:G, :], -1.0, spare[:, 0:1], ALU.mult, ALU.add) \
              .then_inc(spare_ready, 1)
            dve.wait_ge(rel_ready, 1)
            dve.wait_ge(weights_ready, 1)
            dve.wait_ge(spare_ready, 1)

            lanes = [P, LANES, WINDOW]

            def window_match(o, i, k, d, done):
                nc.vector.tensor_tensor(o, iota_w[:, :].rearrange("p (a w) -> p a w", a=1).to_broadcast(lanes),
                                        rel_t[:, bass.ds(group(i, k, d), 1), :]
                                        .rearrange("p a j -> p j a").to_broadcast(lanes),
                                        ALU.is_equal).then_inc(done, 1)

            def window_start(i, k, d):
                g = group(i, k, d)
                late = isinstance(g, int) and g >= EARLY_GROUPS
                return dve.value_load((late_row if late else base_row)[0:1, bass.ds(g, 1)],
                                      min_val=0, max_val=N - 1)

            def step0(i, k, live):
                g, b = group(i, k), k % 2
                dve.wait_ge(src_spread, g + 1)
                if live(2):
                    dve.wait_ge(mix_summed, g - 1)
                nc.vector.tensor_tensor(equal[:, b, :, :],
                                        ps_cap[:, b, :].rearrange("p (e j) -> p j e", j=LANES),
                                        idx_t[:, bass.ds(g, 1), :].rearrange("p a j -> p j a")
                                        .to_broadcast([P, LANES, P]), ALU.is_equal).then_inc(equal_done, 1)
                window_match(oh0[:, b, :, :], i, k, 0, oh0_done)
                dve.wait_ge(equal_done, g + 1)
                for j in range(LANES):
                    nc.vector.tensor_tensor_reduce(earlier[:, j, :], equal[:, b, j, :], below[:, :], 1.0, 0.0,
                                                   ALU.mult, ALU.add, count[:, b, j:j + 1]) \
                      .then_inc(count_done, 1)
                dve.wait_ge(oh0_done, g + 1)
                nc.vector.tensor_tensor(ohw[:, b, :, :], oh0[:, b, :, :],
                                        w_t[:, bass.ds(g, 1), :].rearrange("p a j -> p j a")
                                        .to_broadcast(lanes), ALU.mult).then_inc(ohw_done, 1)
                dve.wait_ge(count_done, (g + 1) * LANES)
                nc.vector.scalar_tensor_tensor(out=away[:, b, :], in0=count[:, b, :], scalar=1.0,
                                               in1=to_spare[:, bass.ds(g, 1), :].rearrange("p a j -> p (a j)"),
                                               op0=ALU.min, op1=ALU.mult).then_inc(away_done, 1)
                if live(SLOTS):
                    dve.wait_ge(scatter_open, (g - SLOTS + 2) * LANES)
                dve.wait_ge(away_done, g + 1)
                nc.vector.tensor_tensor(idx0[:, k, :], away[:, b, :],
                                        idx_t[:, bass.ds(g, 1), :].rearrange("p a j -> p (a j)"),
                                        ALU.add).then_inc(idx0_ready, 1)

            pipeline(dve, step0, 0)

            dve.wait_ge(h_done, NBLK - NCH)
            dve.wait_ge(h_last, NCH)
            nc.vector.scalar_tensor_tensor(out=xs[:, :, :], in0=hs[:, :, :], scalar=0.25, in1=xs[:, :, :],
                                           op0=ALU.mult, op1=ALU.add).then_inc(xh_done, 1)
            dve.wait_ge(prev_loaded, 16 * 3)
            nc.vector.tensor_tensor(same_f[:, :], dst_g[:, :], prev_g[:, :], ALU.is_equal).then_inc(same_done, 1)
            dve.wait_ge(same_done, 1)
            nc.vector.tensor_scalar(cap_g[:, :], same_f[:, :], 2 * BIG, -BIG, ALU.mult, ALU.add) \
              .then_inc(caps_ready, 1)
            dve.wait_ge(caps_ready, 1)
            nc.vector.tensor_tensor(same_f[:, :], prev_g[:, :], dst_g[:, :], ALU.subtract).then_inc(reach_done, 1)
            dve.wait_ge(reach_done, 1)
            nc.vector.scalar_tensor_tensor(out=src_f[:, :], in0=dst_f[:, :], scalar=1.0, in1=same_f[:, :],
                                           op0=ALU.add, op1=ALU.min).then_inc(reach_done, 1)
            dve.wait_ge(reach_done, 2)
            nc.vector.scalar_tensor_tensor(out=same_f[:, :], in0=rel_f[:, :], scalar=float(1 - WINDOW),
                                           in1=src_f[:, :], op0=ALU.add, op1=ALU.max).then_inc(reach_done, 1)
            dve.wait_ge(reach_done, 3)
            nc.vector.tensor_reduce(reach[:, :], same_f[:, :], mybir.AxisListType.X, ALU.max) \
              .then_inc(reach_done, 1)
            dve.wait_ge(mlp_turned, 1)
            nc.vector.tensor_copy(w_tr[:, :], ps_sum[:, 0, 0:D]).then_inc(mlp_ready, 1)
            dve.wait_ge(w_loaded, 16 * 3)
            dve.wait_ge(idents_ready, 2)
            nc.vector.tensor_scalar(scale_diag[:, :], ident[:, :], scale_col[:, 0:1], None, ALU.mult) \
              .then_inc(mlp_ready, 1)
            nc.vector.memset(acc_t[:, :, :], 0.0).then_inc(acc_zero, 1)
            dve.wait_ge(reach_turned, 1)
            nc.vector.tensor_reduce(furthest[:, :], ps_sum[0:1, 1, 0:G], mybir.AxisListType.X, ALU.max) \
              .then_inc(reach_done, 1)
            nc.vector.tensor_scalar(lack[:, :], base_row[:, EARLY_GROUPS:EARLY_GROUPS + 1], -1.0,
                                    float(EARLY_NODES), ALU.mult, ALU.add).then_inc(reach_done, 1)
            nc.vector.tensor_scalar(late_row[:, :], base_row[:, :], EARLY_NODES, None, ALU.max) \
              .then_inc(reach_done, 1)
            dve.wait_ge(reach_done, 7)
            nc.vector.tensor_tensor(furthest[:, :], furthest[:, :], lack[:, :], ALU.max).then_inc(reach_done, 1)
            dve.wait_ge(reach_done, 8)
            nc.vector.tensor_scalar(beyond[:, :], furthest[:, :], 0.0, 1.0, ALU.max, ALU.min) \
              .then_inc(beyond_ready, 1)
            dve.wait_ge(acc_zero, 1)
            dve.wait_ge(xh_done, 1)
            dve.wait_ge(side0_loaded, 16 * NBLK)
            nc.vector.scalar_tensor_tensor(out=xs[:, :, :], in0=rs[:, :, :], scalar=0.75, in1=xs[:, :, :],
                                           op0=ALU.mult, op1=ALU.add).then_inc(side0_done, 1)
            dve.wait_ge(side0_done, 1)

            for c, ch in enumerate(CHUNKS):
                a0, a1 = ch[0], ch[-1] + 1
                n = a1 - a0
                dve.wait_ge(sides_done, c + 1)
                nc.vector.scalar_tensor_tensor(out=xs[:, a0:a1, :], in0=triple[:, c % 2, 0:n, :],
                                               scalar=0.75, in1=xs[:, a0:a1, :], op0=ALU.mult,
                                               op1=ALU.add).then_inc(x1_done, 1)
                dve.wait_ge(x1_done, c + 1)
                norm_stats(c, ch, stats1_done, aggr1_done)
                if c >= 1:
                    norm_scale(c - 1, CHUNKS[c - 1], std1_done, rstd1_done, shift1_done)
            norm_scale(NCH - 1, CHUNKS[-1], std1_done, rstd1_done, shift1_done)
            dve.wait_ge(h2_done, NBLK)
            nc.vector.tensor_tensor(rs[:, :, :], xs[:, :, :], hs[:, :, :], ALU.add).then_inc(r_done, 1)

            def step(i, k, live):
                if live(2):
                    g, b = group(i, k, 2), k % 2
                    dve.wait_ge(b_done, g + 1)
                    if live(4):
                        dve.wait_ge(sums_done, g - 1)
                    nc.vector.tensor_tensor(ec[:, b, 0, :, :], m[:, (k - 2) % SLOTS, :, :], ps_b[:, b, :, :],
                                            ALU.subtract).then_inc(sub_done, 1)
                if live(1):
                    g, b = group(i, k, 1), (k - 1) % 2
                    now = mx[:, (k - 1) % 4, :]
                    dve.wait_ge(evac_done, g + 1)
                    dve.wait_ge(caps_spread, g + 1)
                    if live(5):
                        dve.wait_ge(b_done, g - 3)
                    before = mx[:, (k - 2) % 4, GROUP - 1:GROUP] if live(2) else -BIG
                    nc.vector.tensor_tensor_scan(now, ps_cap[:, 0, :], mt[:, b, :], before,
                                                 ALU.min, ALU.max).then_inc(scan_done, 1)
                if live(2):
                    window_match(oh[:, k % 2, :, :], i, k, 2, oh_done)
                if live(1):
                    dve.wait_ge(scan_done, g + 1)
                    back = mx[:, (k - 1) % 4, GROUP - 2::-1]
                    nc.vector.tensor_tensor_scan(back, ps_cap[:, 0, GROUP - 1:0:-1], back,
                                                 mx[:, (k - 1) % 4, GROUP - 1:GROUP], ALU.min, ALU.max) \
                      .then_inc(rev_done, 1)
                if live(2):
                    b2 = k % 2
                    dve.wait_ge(exp_done, group(i, k, 2) + 1)
                    nc.vector.tensor_tensor(ec[:, b2, 1, :, :], m[:, (k - 2) % SLOTS, :, :],
                                            ec[:, b2, 0, :, :], ALU.mult).then_inc(mul_done, 1)
                if live(1):
                    c = (k - 1) % 4
                    dve.wait_ge(rev_done, g + 1)
                    if live(5):
                        dve.wait_ge(fac_done, g - 3)
                    first = mx[:, c, 0:1]
                    nc.vector.scalar_tensor_tensor(out=drop[:, c:c + 1], in0=first,
                                                   scalar=(mx[:, (k - 2) % 4, GROUP - 1:GROUP] if live(2)
                                                           else 0.0),
                                                   in1=first, op0=ALU.min, op1=ALU.subtract) \
                      .then_inc(drop_done, 1)
                if live(3):
                    g, b, c = group(i, k, 3), (k - 3) % 2, (k - 3) % 4
                    start = window_start(i, k, 3)
                    dve.wait_ge(fac_done, g + 1)
                    if live(4):
                        dve.wait_ge(added, g)
                    head = acc_t[:, :, bass.ds(start, 1)]
                    nc.vector.tensor_scalar(head, head, fac[:, c:c + 1], None, ALU.mult).then_inc(rescaled, 1)
                    dve.wait_ge(rescaled, g + 1)
                    dve.wait_ge(sums_done, g + 1)
                    cols = acc_t[:, :, bass.ds(start, WINDOW)]
                    nc.vector.tensor_tensor(cols, cols, ps_sum[:, b, 0:2 * WINDOW]
                                            .rearrange("p (q w) -> p q w", q=2), ALU.add).then_inc(added, 1)

            def aggregate(c, ch):
                n0, n1 = ch[0] * NP_, (ch[-1] + 1) * NP_
                dve.wait_ge(guess_done, guesses(c))
                nc.vector.tensor_tensor(acc_t[:, 0, n0:n1], acc_t[:, 0, n0:n1], guess[:, n0:n1], ALU.mult) \
                  .then_inc(check_done, 1)
                if c < EARLY:
                    nc.vector.tensor_tensor(acc_t[:, 1, n0:n1], acc_t[:, 1, n0:n1], guess[:, n0:n1], ALU.mult) \
                      .then_inc(quot_done, 1)
                dve.wait_ge(check_done, c + 1)
                dve.wait_ge(quot_done, c + 1)
                nc.vector.scalar_tensor_tensor(out=acc_t[:, 1, n0:n1], in0=acc_t[:, 0, n0:n1], scalar=2.0,
                                               in1=acc_t[:, 1, n0:n1], op0=ALU.subtract, op1=ALU.mult,
                                               reverse0=True).then_inc(agg_done, 1)

            def finish(c, ch, back_sem, done):
                a0, a1 = ch[0], ch[-1] + 1
                dve.wait_ge(back_sem, c + 1)
                nc.vector.tensor_tensor(rs[:, a0:a1, :], rs[:, a0:a1, :],
                                        back_bank(c, (a1 - a0) * D).rearrange("p (a c) -> p a c", c=D),
                                        ALU.add).then_inc(done, 1)

            def early(t):
                if (t - 3) // 2 in range(EARLY) and t % 2 == 1:
                    aggregate((t - 3) // 2, OUTS[(t - 3) // 2])

            dve.wait_ge(r_done, 1)
            pipeline(dve, step, 3, early=early)

            for c in range(EARLY):
                finish(c, OUTS[c], back_done, out_done)
            for c in range(EARLY, NOUT):
                aggregate(c, OUTS[c])
            for c in range(EARLY, NOUT):
                finish(c, OUTS[c], back_done, out_done)

            with dve.If(out_of_windows(dve)):
                def column(table, n):
                    return table[:, bass.ds(n, 1)]

                def end_of(q, e):
                    return dve.value_load(ends[0:1, q, bass.ds(e, 1)], min_val=0, max_val=N - 1)

                def take_nodes(before):
                    for c, ch in enumerate(CHUNKS):
                        n0, n1 = ch[0] * NP_, (ch[-1] + 1) * NP_
                        dve.wait_ge(cols_turned, before + c + 1)
                        nc.vector.tensor_copy(h_cols[:, n0:n1], ps_mt[:, c % 2, 0:n1 - n0]) \
                          .then_inc(cols_taken, 1)

                nc.vector.memset(acc_t[:, :, :], 0.0)
                take_nodes(0)
                dve.drain().then_inc(staging_free, 1)

                def add_messages(g, n):
                    dve.wait_ge(edges_loaded, loads_count(0, g))
                    dve.sem_inc(loop_open, 1)
                    with dve.Fori(0, n) as e:
                        s, d = end_of(0, e), end_of(1, e)
                        dve.drain()
                        nc.vector.scalar_tensor_tensor(
                            out=acc_t[:, 0, bass.ds(s, 1)], in0=column(h_cols, d), scalar=column(weights, e),
                            in1=acc_t[:, 0, bass.ds(s, 1)], op0=ALU.mult, op1=ALU.add)
                    dve.drain().then_inc(staging_free, 1)

                each_group(dve, add_messages)
                dve.drain().then_inc(side_summed, 1)

                dve.wait_ge(again_loaded, 32)
                nc.vector.scalar_tensor_tensor(out=xs[:, :, :], in0=hs[:, :, :], scalar=0.25, in1=xs[:, :, :],
                                               op0=ALU.mult, op1=ALU.add)
                dve.drain()
                for c, ch in enumerate(CHUNKS):
                    a0, a1 = ch[0], ch[-1] + 1
                    dve.wait_ge(rows_turned, c + 1)
                    nc.vector.scalar_tensor_tensor(
                        out=xs[:, a0:a1, :],
                        in0=ps_cap[0:NP_, c % 2, 0:(a1 - a0) * D].rearrange("p (a c) -> p a c", c=D),
                        scalar=0.75, in1=xs[:, a0:a1, :], op0=ALU.mult, op1=ALU.add).then_inc(rows_taken, 1)
                dve.drain()
                for a in range(NBLK):
                    nc.vector.bn_stats(stats[:, a, :], xs[:, a, :])
                dve.drain()
                for a in range(NBLK):
                    nc.vector.bn_aggr(meanvar[:, a, :], stats[:, a, :])
                dve.drain().then_inc(var_ready, 1)
                dve.wait_ge(root_ready, 1)
                nc.vector.reciprocal(rstd[:, :], std[:, :])
                dve.drain()
                nc.vector.scalar_tensor_tensor(out=shift[:, :], in0=meanvar[:, :, 0], scalar=-1.0,
                                               in1=rstd[:, :], op0=ALU.mult, op1=ALU.mult)
                dve.drain()
                for a in range(NBLK):
                    nc.vector.tensor_scalar(hs[:, a, :], xs[:, a, :], rstd[:, a:a + 1], shift[:, a:a + 1],
                                            ALU.mult, ALU.add)
                dve.drain()
                nc.vector.tensor_scalar(hs[:, :, :], hs[:, :, :], 0.0, None, ALU.max)
                dve.drain().then_inc(h2_again, 1)
                nc.vector.tensor_tensor(rs[:, :, :], xs[:, :, :], hs[:, :, :], ALU.add)
                take_nodes(NCH)
                nc.vector.memset(acc_t[:, :, :], 0.0)
                nc.vector.memset(top, -BIG)
                dve.drain().then_inc(staging_free, 1)

                def take_edges(t, g, n):
                    dve.wait_ge(edges_loaded, loads_count(t, g))
                    dve.wait_ge(ea_turned, g + (1 + (t - 1) * G))
                    nc.vector.tensor_copy(ea_cols[:, 0:n],
                                          ps_b[:, 0, :, :].rearrange("p j e -> p (j e)")[:, 0:n])
                    dve.drain()

                def raise_top(g, n):
                    take_edges(1, g, n)
                    with dve.Fori(0, n) as e:
                        s, d = end_of(0, e), end_of(1, e)
                        dve.drain()
                        nc.vector.scalar_tensor_tensor(out=column(top, d), in0=column(h_cols, s),
                                                       scalar=column(ea_cols, e), in1=column(top, d),
                                                       op0=ALU.add, op1=ALU.max)
                    dve.drain().then_inc(staging_free, 1)

                each_group(dve, raise_top)
                dve.drain().then_inc(staging_free, 1)

                def add_terms(g, n):
                    take_edges(2, g, n)
                    with dve.Fori(0, n) as e:
                        s, d = end_of(0, e), end_of(1, e)
                        nc.vector.scalar_tensor_tensor(out=column(terms[:, 1, :], e), in0=column(h_cols, s),
                                                       scalar=column(ea_cols, e), in1=column(top, d),
                                                       op0=ALU.add, op1=ALU.subtract)
                    dve.drain().then_inc(z_ready, 1)
                    dve.wait_ge(e_ready, g + 1)
                    nc.vector.tensor_tensor(terms[:, 1, 0:n], terms[:, 1, 0:n], terms[:, 0, 0:n], ALU.mult)
                    with dve.Fori(0, n) as e:
                        d = end_of(1, e)
                        sums = acc_t[:, :, bass.ds(d, 1)]
                        dve.drain()
                        nc.vector.tensor_tensor(sums, sums, terms[:, :, bass.ds(e, 1)], ALU.add)
                    dve.drain().then_inc(staging_free, 1)

                each_group(dve, add_terms)

                total, weighted = acc_t[:, 0, 0:N], acc_t[:, 1, 0:N]
                nc.vector.tensor_tensor(top, top, total, ALU.mult)
                dve.drain()
                nc.vector.tensor_tensor(weighted, weighted, top, ALU.add)
                nc.vector.tensor_scalar(total, total, TINY, None, ALU.max)
                dve.drain()
                nc.vector.reciprocal(total, total)
                dve.drain()
                nc.vector.tensor_tensor(weighted, weighted, total, ALU.mult)
                dve.drain().then_inc(agg_again, 1)
                for c, ch in enumerate(OUTS):
                    finish(c, ch, back_again, out_again)


_INS = ['x', 'src', 'dst', 'edge_attr_128', 'edge_weight', 'L1_gnn_mlp_w', 'L1_gnn_mlp_b', 'L1_gnn_scale']
_OUTS = [((3125, 128), 'float32')]


def kernel(**inputs):
    import numpy as _np
    import concourse.bacc as _bacc
    from concourse import mybir as _mybir
    from concourse.bass_utils import run_bass_kernel_spmd as _run

    nc = _bacc.Bacc("TRN2", target_bir_lowering=False, num_devices=1)
    arrays, args = {}, []
    for name in _INS:
        a = _np.ascontiguousarray(inputs[name])
        arrays[f"in_{name}_dram"] = a
        args.append(nc.dram_tensor(f"in_{name}_dram", a.shape, _mybir.dt.from_np(a.dtype),
                                   kind="ExternalInput").ap())
    for i, (shape, dtype) in enumerate(_OUTS):
        dt = _mybir.dt.from_np(_np.dtype(dtype))
        args.append(nc.dram_tensor(f"out_{i}_dram", shape, dt, kind="ExternalOutput").ap())
    gnn_kernel(nc, *args)
    r = _run(nc, [arrays], core_ids=[0])
    return r.results[0]["out_0_dram"]
```
